# Optimizing a Trainium2 kernel written in Bass

```python
import numpy as np
import jax
import jax.numpy as jnp

def _softmax(x, axis=-1):
    return jax.nn.softmax(x, axis=axis)

def _gelu(x):
    return jax.nn.gelu(x, approximate=True)

def _silu(x):
    return jax.nn.silu(x)

def _sigmoid(x):
    return jax.nn.sigmoid(x)

def _layernorm(x, axis=-1, eps=1e-05):
    m = jnp.mean(x, axis=axis, keepdims=True)
    v = jnp.var(x, axis=axis, keepdims=True)
    return (x - m) / jnp.sqrt(v + eps)

def _scatter_add(tgt, idx, src, axis=0):
    return tgt.at[idx].add(src)

def _segment_sum(src, seg, n):
    return jax.ops.segment_sum(src, seg, n)
kernel_name = 'mk_conv_preact_d2_conv_nchw256_r4_8675ad'

def setup_inputs(seed: int=0):
    np.random.seed(seed)
    _w = jnp.asarray

    def _rec_inputs():
        import jax
        import jax.numpy as jnp
        _gk = jax.random.key(seed)
        x = -0.0002091 + 1 * jax.random.normal(jax.random.fold_in(_gk, 1), (32, 64, 56, 56), jnp.float32)
        return x
    x = _rec_inputs()

    def _L0_conv_setup():
        import jax, jax.numpy as jnp
        import numpy as np
        OUT_CH = 64
        IN_CH = 64
        K = 3
        STRIDE = 1
        PAD = 1
        key = jax.random.key(seed)
        k_x, k_w, k_s = jax.random.split(key, 3)
        x = jax.random.normal(k_x, (32, IN_CH, 56, 56), dtype=jnp.float32)
        weight = jax.random.normal(k_w, (OUT_CH, IN_CH, K, K), dtype=jnp.float32) * 0.05
        scale = jnp.full((OUT_CH,), 0.001, dtype=jnp.float32)
        return {'x': x, 'weight': weight, 'scale': scale}
    _L0_conv_all = _L0_conv_setup()
    _L0_conv_in = {k: v for k, v in _L0_conv_all.items() if k in ('weight', 'scale')}
    del _L0_conv_all

    def _L1_conv_setup():
        import jax, jax.numpy as jnp
        import numpy as np
        K = 7
        G = 16
        P = K // 2
        EPS = 1e-05

        def _weight_norm(v, g):
            return v * (g / jnp.linalg.norm(v, axis=1))[:, None]
        key = jax.random.key(seed)
        ks = jax.random.split(key, 4)
        B, C, H, W = (8, 64, 16, 16)
        CR = C // 4
        KKG = K * K * G
        return {'x': jax.random.normal(ks[0], (B, C, H, W), jnp.float32), 'v_reduce': jax.random.normal(ks[1], (CR, C), jnp.float32) * 0.05, 'g_reduce': jnp.ones((CR,), jnp.float32), 'b_reduce': jnp.zeros((CR,), jnp.float32), 'bn_gamma': jnp.ones((CR,), jnp.float32), 'bn_beta': jnp.zeros((CR,), jnp.float32), 'bn_mean': jnp.zeros((CR,), jnp.float32), 'bn_var': jnp.ones((CR,), jnp.float32), 'v_span': jax.random.normal(ks[2], (KKG, CR), jnp.float32) * 0.05, 'g_span': jnp.ones((KKG,), jnp.float32), 'b_span': jnp.zeros((KKG,), jnp.float32)}
    _L1_conv_all = _L1_conv_setup()
    _L1_conv_in = {k: v for k, v in _L1_conv_all.items() if k in ('v_reduce', 'g_reduce', 'b_reduce', 'bn_gamma', 'bn_beta', 'bn_mean', 'bn_var', 'v_span', 'g_span', 'b_span')}
    del _L1_conv_all
    return {'x': x, 'L0_conv_weight': _L0_conv_in['weight'], 'L0_conv_scale': _L0_conv_in['scale'], 'L1_conv_v_reduce': _L1_conv_in['v_reduce'], 'L1_conv_g_reduce': _L1_conv_in['g_reduce'], 'L1_conv_b_reduce': _L1_conv_in['b_reduce'], 'L1_conv_bn_gamma': _L1_conv_in['bn_gamma'], 'L1_conv_bn_beta': _L1_conv_in['bn_beta'], 'L1_conv_bn_mean': _L1_conv_in['bn_mean'], 'L1_conv_bn_var': _L1_conv_in['bn_var'], 'L1_conv_v_span': _L1_conv_in['v_span'], 'L1_conv_g_span': _L1_conv_in['g_span'], 'L1_conv_b_span': _L1_conv_in['b_span']}

def reference(x, L0_conv_weight, L0_conv_scale, L1_conv_v_reduce, L1_conv_g_reduce, L1_conv_b_reduce, L1_conv_bn_gamma, L1_conv_bn_beta, L1_conv_bn_mean, L1_conv_bn_var, L1_conv_v_span, L1_conv_g_span, L1_conv_b_span):
    import jax
    import jax.numpy as jnp

    def _L0_conv_ref(x, weight, scale):
        import jax, jax.numpy as jnp
        import numpy as np
        OUT_CH = 64
        IN_CH = 64
        K = 3
        STRIDE = 1
        PAD = 1
        xb = jnp.sign(x)
        wb = jnp.sign(weight)
        y = jax.lax.conv_general_dilated(xb, wb, window_strides=(STRIDE, STRIDE), padding=[(PAD, PAD), (PAD, PAD)], rhs_dilation=(1, 1), dimension_numbers=('NCHW', 'OIHW', 'NCHW'))
        return y * scale[None, :, None, None]

    def _L1_conv_ref(x, v_reduce, g_reduce, b_reduce, bn_gamma, bn_beta, bn_mean, bn_var, v_span, g_span, b_span):
        import jax, jax.numpy as jnp
        import numpy as np
        K = 7
        G = 16
        P = K // 2
        EPS = 1e-05

        def _weight_norm(v, g):
            return v * (g / jnp.linalg.norm(v, axis=1))[:, None]
        B, C, H, W = x.shape
        D = C // G
        w_r = _weight_norm(v_reduce, g_reduce)
        r = jnp.einsum('oc,bchw->bohw', w_r, x) + b_reduce[:, None, None]
        scale = (bn_gamma / jnp.sqrt(bn_var + EPS))[:, None, None]
        r = jax.nn.relu((r - bn_mean[:, None, None]) * scale + bn_beta[:, None, None])
        w_s = _weight_norm(v_span, g_span)
        ker = jnp.einsum('oc,bchw->bohw', w_s, r) + b_span[:, None, None]
        ker = ker.reshape(B, K, K, G, H, W).transpose(0, 3, 1, 2, 4, 5)
        ker = ker.reshape(B, G, K * K, H, W)
        xp = jnp.pad(x, ((0, 0), (0, 0), (P, P), (P, P)))
        xp = xp.reshape(B, G, D, H + 2 * P, W + 2 * P)
        out = jnp.zeros((B, G, D, H, W), x.dtype)
        for ki in range(K):
            for kj in range(K):
                out = out + xp[:, :, :, ki:ki + H, kj:kj + W] * ker[:, :, ki * K + kj][:, :, None]
        return out.reshape(B, C, H, W)

    def _gn(v, G=32, eps=1e-05):
        B_, C_, H_, W_ = v.shape
        g = v.reshape(B_, G, C_ // G, H_, W_)
        m = jnp.mean(g, axis=(2, 3, 4), keepdims=True)
        s = jnp.var(g, axis=(2, 3, 4), keepdims=True)
        return ((g - m) / jnp.sqrt(s + eps)).reshape(v.shape)

    def _ln_c(v, eps=1e-06):
        m = jnp.mean(v, axis=1, keepdims=True)
        s = jnp.var(v, axis=1, keepdims=True)
        return (v - m) / jnp.sqrt(s + eps)

    def _ln_t(v, eps=1e-05):
        m = jnp.mean(v, axis=-1, keepdims=True)
        s = jnp.var(v, axis=-1, keepdims=True)
        return (v - m) / jnp.sqrt(s + eps)

    def _to_tokens(v):
        B_, C_, H_, W_ = v.shape
        return v.reshape(B_, C_, H_ * W_).transpose(0, 2, 1)

    def _from_tokens(t, like):
        B_, C_, H_, W_ = like.shape
        return t.transpose(0, 2, 1).reshape(B_, C_, H_, W_)
    x = x + _L0_conv_ref(_gn(x), L0_conv_weight, L0_conv_scale)
    x = x + _L1_conv_ref(_gn(x), L1_conv_v_reduce, L1_conv_g_reduce, L1_conv_b_reduce, L1_conv_bn_gamma, L1_conv_bn_beta, L1_conv_bn_mean, L1_conv_bn_var, L1_conv_v_span, L1_conv_g_span, L1_conv_b_span)
    return x

_drawn_inputs = setup_inputs


def setup_inputs(seed=0):
    import zlib

    import numpy as np

    out = dict(_drawn_inputs(seed))
    spreads = {'L0_conv_scale': (0.0010000000474974513, 0.2),
     'L1_conv_g_reduce': (1.0, 0.2),
     'L1_conv_b_reduce': (0.0, 0.1),
     'L1_conv_bn_gamma': (1.0, 0.2),
     'L1_conv_bn_beta': (0.0, 0.1),
     'L1_conv_bn_mean': (0.0, 0.1),
     'L1_conv_bn_var': (1.0, 0.2),
     'L1_conv_g_span': (1.0, 0.2),
     'L1_conv_b_span': (0.0, 0.1)}
    factors = {}
    for name, (base, spread) in spreads.items():
        noise = np.random.default_rng([zlib.crc32(name.encode()), seed]).standard_normal(out[name].shape)
        drawn = base * np.exp(spread * noise) if base else spread * noise
        out[name] = jnp.asarray(drawn.astype(out[name].dtype))
    for name, factor in factors.items():
        out[name] = (out[name] * factor).astype(out[name].dtype)
    return out
```

```python
from contextlib import ExitStack

import concourse.bass as bass
from concourse import mybir

F32 = mybir.dt.float32
F16 = mybir.dt.float16
BF16 = mybir.dt.bfloat16
U32 = mybir.dt.uint32
ALU = mybir.AluOpType
ACT = mybir.ActivationFunctionType
AX = mybir.AxisListType

B, C, H, W = 32, 64, 56, 56
PAIRS = B // 2
HW = H * W
GROUPS, GC = 16, 4
O = 16
K, PAD = 7, 3
TAPS = K * K
PY, PX = 2, 8
POS = PY * PX
IY, IX = PY + K - 1, PX + K - 1
PATCH = IY * IX
STRIPS = W // PX
ROWS = H + 2 * PAD
STRIP = ROWS * IX
Q = 4
JY = H // (PY * Q)
J = JY * STRIPS
UNIT = 2 * J * GC
HALF = J * GC
CR = 8
CHUNKS = H // CR
CW = CR * W
XS, WS = 256.0, 1024.0
EPS = 1e-5
TINY = 1e-30

C_ID, C_SEL = 0, 128
C_G = C_SEL + POS * PATCH
C_E = C_G + 128
C_R = C_E + 56
C_N = C_R + 2 * 64
P_SCALE, P_G, P_B, P_GAMMA, P_BETA, P_MEAN, P_VAR, P_VT = range(8)
P_ROW = P_VT + O
P_CONV = P_ROW + C
P_N = P_CONV + 9 * C

LOADS, ZEROS = 16 * 9, 4
FRONT_M, BACK_M = CHUNKS + 3, JY
T_ALL = 2 * Q * JY
T_ON_DVE = [n % 5 in (0, 2, 4) for n in range(T_ALL)]
CONV_AFTER = {3: (0,), 4: (1,), 5: (2, 3), 6: (4, 5), 7: (6,)}


def build(nc, x, consts, params, span, gb_all, vr_all, out, pairs=PAIRS):
    xv = x.rearrange("(p b) c h w -> p (b c) (h w)", b=2)
    ov = out.rearrange("(p b) c h w -> p (b c) (h w)", b=2)
    steps = pairs - 1

    with ExitStack() as ctx:
        def sb(name, shape, dt=F32):
            return ctx.enter_context(nc.sbuf_tensor(name, shape, dt))

        def sem(name):
            return ctx.enter_context(nc.semaphore(name))

        X = sb("patches", [128, 2 * Q * J * 128], F16)
        wspan = sb("wspan", [128, 2 * GROUPS * PY * 128], F16)
        wbias = sb("wbias", [128, 2 * GROUPS, 48], F16)
        S = sb("strips", [128, 2, STRIPS * STRIP], F16)
        xs = sb("xs", [128, 2 * HW])
        xn = sb("xn", [128, 2, H * IX])
        R = sb("relu", [128, PY, Q, 2, J])
        prod = sb("prod", [128, Q, PY * UNIT])
        osb = sb("osb", [128, J, C])
        ident = sb("ident", [128, 128], F16)
        gmat = sb("gmat", [128, 128])
        esum = sb("esum", [128, 56])
        back = sb("back", [128, 2, 64])
        convw = sb("convw", [128, 9, 128], BF16)
        wred = sb("wred", [128, 2, 240], F16)
        scale = sb("scale", [128, 1])
        red_scale = sb("red_scale", [128, 1])
        red_bias = sb("red_bias", [128, 1])
        alpha = sb("alpha", [128, 1])
        sm = sb("small", [128, 64])
        bn = sb("bn", [128, CHUNKS, 6])
        mv = sb("mv", [128, 2])
        sgn = S[:, 1, 0:(H + 2) * (W + 2)].bitcast(BF16)
        sgn3 = sgn.rearrange("p (h w) -> p h w", w=W + 2)

        Ybank = [ctx.enter_context(nc.psum_tensor(f"ybank{i}", [128, PY, 512], F32)) for i in range(2)]
        Obank = [ctx.enter_context(nc.psum_tensor(f"obank{i}", [128, 512], F32)) for i in range(2)]
        Mbank = [ctx.enter_context(nc.psum_tensor(f"mbank{i}", [128, 512], F32)) for i in range(2)]

        Xv = X[:].rearrange("k (l q j p) -> k l q j p", l=2, q=Q, p=128)
        Wv = wspan[:].rearrange("k (l g d m) -> k l g d m", l=2, g=GROUPS, d=PY)

        setup_loaded = sem("setup_loaded")
        zeroed = sem("zeroed")
        setup_sqrt_in = sem("setup_sqrt_in")
        setup_sqrt_out = sem("setup_sqrt_out")
        convw_ready = sem("convw_ready")
        taps_ready = sem("taps_ready")
        sel_ready = sem("sel_ready")
        sel_read = sem("sel_read")
        chain = sem("chain")
        x_loaded = sem("x_loaded")
        stored = sem("stored")
        sum_ready = sem("sum_ready")
        m_ready = sem("m_ready")
        m_read = sem("m_read")
        nmean_ready = sem("nmean_ready")
        sgn_zeroed = sem("sgn_zeroed")
        sgn_ready = sem("sgn_ready")
        stats_ready = sem("stats_ready")
        var_ready = sem("var_ready")
        std_ready = sem("std_ready")
        affine_ready = sem("affine_ready")
        low_zeroed = sem("low_zeroed")
        high_strip = sem("high_strip")
        low_strip = sem("low_strip")
        r_ready = sem("r_ready")
        r_done = sem("r_done")
        t_ready = sem("t_ready")
        t_act = sem("t_act")
        t_dve = sem("t_dve")
        y_ready = sem("y_ready")
        prod_done = sem("prod_done")
        osum_done = sem("osum_done")
        o_ready = sem("o_ready")
        o_done = sem("o_done")
        out_added = sem("out_added")

        def slot(p):
            return xs[:, bass.ds((p % 2) * HW, HW)]

        def front_use(p, k):
            if isinstance(p, int):
                return k if p == 0 else FRONT_M + (FRONT_M + BACK_M) * (p - 1) + k
            return (p - 1) * (FRONT_M + BACK_M) + FRONT_M + k

        def back_use(p, k, last):
            return p * (FRONT_M + BACK_M) + (FRONT_M if last else 2 * FRONT_M) + k

        def known(eng, value):
            return value if isinstance(value, int) else eng.to_reg(value)

        def tbank(n):
            return Ybank[(n % 4) // 2][:, n % 2, 0:STRIPS * 64].bitcast(F16)

        def tplace(n):
            return n // (Q * JY), n // JY % Q, n % JY

        def strip_range(s):
            return (PAD if s == 0 else 0), (IX - PAD if s == STRIPS - 1 else IX)

        def strip(part, s):
            return S[:, part, s * STRIP + PAD * IX:s * STRIP + (PAD + H) * IX].rearrange("p (h w) -> p h w", w=IX)

        def xn3(s):
            return xn[:, s % 2, :].rearrange("p (h w) -> p h w", w=IX)

        def patch_rows(part, q, jy):
            return Xv[0:PATCH, part, q, STRIPS * jy:STRIPS * (jy + 1), :].rearrange("k j p -> k (j p)")

        DVE_BEFORE = [sum(T_ON_DVE[:n]) for n in range(T_ALL + 1)]
        N_DVE, N_ACT = DVE_BEFORE[T_ALL], T_ALL - DVE_BEFORE[T_ALL]

        tmp = X[:].bitcast(F32)
        t_id, t_sel = tmp[:, 0:128], tmp[0:TAPS, 128:128 + POS * PATCH]
        t_span = tmp[0:TAPS, 2048:2048 + GROUPS * (O + 2)]
        t_gb = tmp[:, 2560:2560 + 2 * TAPS * GROUPS]
        t_vr = tmp[:, 4224:4224 + O * C]
        t_par = tmp[:, 5376:5376 + P_N]
        t_sq = tmp[0:TAPS, 6272:6528]
        t_ss = tmp[0:TAPS, 6528:6544]
        t_rt = tmp[0:TAPS, 6560:6576]
        t_rs = tmp[0:TAPS, 6592:6608]
        t_u = tmp[0:TAPS, 6624:6640]
        t_w = tmp[0:TAPS, 6656:6912]
        t_b = tmp[0:TAPS, 6912:6928]
        t_row = tmp[:, 6944:7008]
        t_vw = tmp[:, 7040:7056]
        t_sel16 = X[0:TAPS, 16384:16384 + POS * PATCH]
        t_w16 = X[0:TAPS, 18432:18432 + 512].rearrange("t (l n) -> t l n", l=2)
        t_b16 = X[0:TAPS, 19200:19232].rearrange("t (l n) -> t l n", l=2)

        def col(i):
            return sm[:, i:i + 1]
        (S_SUM, S_NMEAN, S_GM, S_D, S_T, S_VE, S_SD, S_Y, S_U, S_RS, S_NB) = range(11)

        block = ctx.enter_context(nc.Block())

        @block.sync
        def _(sp):
            for dst, src in ((t_id, consts[:, C_ID:C_ID + 128]), (t_sel, consts[0:TAPS, C_SEL:C_G]),
                             (gmat[:], consts[:, C_G:C_E]), (esum[:], consts[:, C_E:C_R]),
                             (back[:].rearrange("p a b -> p (a b)"), consts[:, C_R:C_N]), (t_span, span),
                             (t_par, params), (t_gb, gb_all.broadcast_to((128, 2 * TAPS * GROUPS))),
                             (t_vr, vr_all.broadcast_to((128, O * C)))):
                sp.dma_start(dst, src).then_inc(setup_loaded, 16)
            sp.dma_start(xs[:, 0:HW], xv[0]).then_inc(x_loaded, 16)
            sp.wait_ge(x_loaded, 16)
            sp.dma_start(xs[:, HW:2 * HW], xv[1]).then_inc(x_loaded, 16)

            def step(p, load_next):
                sp.wait_ge(out_added, p + 1)
                sp.dma_start(ov[p], slot(p)).then_inc(stored, 16)
                sp.wait_ge(stored, 16 * (p + 1))
                if load_next:
                    sp.wait_ge(x_loaded, 16 * (p + 2))
                    sp.dma_start(slot(p), xv[p + 2]).then_inc(x_loaded, 16)

            if pairs > 2:
                with sp.Fori(0, pairs - 2) as p:
                    step(p, True)
            step(pairs - 2, False)
            step(pairs - 1, False)

        @block.gpsimd
        def _(pool):
            pool.memset(S[:].rearrange("p l n -> p (l n)").bitcast(U32), 0).then_inc(zeroed, 1)
            pool.memset(wbias[:].rearrange("p a b -> p (a b)").bitcast(U32), 0).then_inc(zeroed, 1)
            pool.memset(wred[:].rearrange("p a b -> p (a b)").bitcast(U32), 0).then_inc(zeroed, 1)
            pool.memset(convw[:].rearrange("p a b -> p (a b)").bitcast(U32), 0).then_inc(zeroed, 1)
            pool.wait_ge(zeroed, ZEROS)

            def front(p):
                transposed = known(pool, T_ALL * p)
                pool.wait_ge(zeroed, ZEROS)
                if not (isinstance(p, int) and p == 0):
                    pool.wait_ge(t_ready, transposed)
                pool.memset(sgn.bitcast(U32), 0).then_inc(sgn_zeroed, 1)
                convolved = known(pool, front_use(p, CHUNKS) + 1)
                pool.wait_ge(zeroed, ZEROS)
                pool.wait_ge(m_ready, convolved)
                pool.memset(S[:, 1, :].bitcast(U32), 0).then_inc(low_zeroed, 1)
                pool.wait_ge(low_zeroed, p + 1)
                for s in range(STRIPS):
                    lo, hi = strip_range(s)
                    pool.wait_ge(high_strip, STRIPS * p + s + 1)
                    pool.tensor_tensor(strip(1, s)[:, :, lo:hi], xn3(s)[:, :, lo:hi], strip(0, s)[:, :, lo:hi],
                                       ALU.subtract).then_inc(low_strip, 1)

            front(0)
            if steps > 0:
                with pool.Fori(0, steps) as i:
                    front(i + 1)

        @block.scalar
        def _(act):
            act.wait_ge(setup_loaded, LOADS)
            act.wait_ge(zeroed, ZEROS)
            for b in range(2):
                act.activation(convw[64 * b:64 * b + 64, :, 64 * b:64 * b + 64],
                               t_par[64 * b:64 * b + 64, P_CONV:P_N].rearrange("p (t o) -> p t o", t=9),
                               ACT.Sign).then_inc(convw_ready, 1)
            act.wait_ge(setup_sqrt_in, 1)
            act.activation(t_rt, t_ss, ACT.Sqrt).then_inc(setup_sqrt_out, 1)
            act.activation(sm[:, 36:38], sm[:, 34:36], ACT.Sqrt).then_inc(setup_sqrt_out, 1)
            act.wait_ge(setup_sqrt_out, 2)
            act.activation(sm[:, 50:51], sm[:, 36:37], ACT.Copy).then_inc(o_done, 1)

            def sign(p):
                turn = known(act, p + 1)
                act.wait_ge(setup_loaded, LOADS)
                act.wait_ge(nmean_ready, turn)
                act.wait_ge(sgn_zeroed, turn)
                act.activation(sgn3[:, 1:H + 1, 1:W + 1], slot(p).rearrange("p (h w) -> p h w", w=W),
                               ACT.Sign, bias=col(S_NMEAN)).then_inc(sgn_ready, 1)

            def root(p):
                act.wait_ge(var_ready, p + 1)
                act.activation(col(S_SD), col(S_VE), ACT.Sqrt).then_inc(std_ready, 1)

            def strips(p):
                act.wait_ge(affine_ready, p + 1)
                if not (isinstance(p, int) and p == 0):
                    act.wait_ge(t_ready, T_ALL * p)
                x3 = slot(p).rearrange("p (h w) -> p h w", w=W)
                for s in range(STRIPS):
                    lo, hi = strip_range(s)
                    src = x3[:, :, PX * s - PAD + lo:PX * s - PAD + hi]
                    read = known(act, STRIPS * p + max(s - 1, 0))
                    act.wait_ge(zeroed, ZEROS)
                    if not (isinstance(read, int) and read == 0):
                        act.wait_ge(low_strip, read)
                    act.activation(xn3(s)[:, :, lo:hi], src, ACT.Identity, bias=col(S_NB), scale=col(S_RS))
                    act.activation(strip(0, s)[:, :, lo:hi], src, ACT.Identity, bias=col(S_NB),
                                   scale=col(S_RS)).then_inc(high_strip, 1)

            def relus(p):
                for dy in range(PY):
                    for b in range(2):
                        act.wait_ge(r_ready, 4 * p + 2 * dy + b + 1)
                        act.activation(R[:, dy, :, b, :],
                                       Ybank[b][:, dy, 0:Q * J].rearrange("m (q j) -> m q j", q=Q),
                                       ACT.Relu, bias=red_bias[:], scale=red_scale[:]).then_inc(r_done, 1)

            def patches(p):
                for n in range(T_ALL):
                    if not T_ON_DVE[n]:
                        part, q, jy = tplace(n)
                        act.wait_ge(t_ready, T_ALL * p + n + 1)
                        act.activation(patch_rows(part, q, jy), tbank(n)[0:PATCH, :], ACT.Copy).then_inc(t_act, 1)

            def gather(p, G):
                act.wait_ge(o_ready, 8 * p + G + 1)
                act.activation(osb[:, :, 2 * GC * G:2 * GC * (G + 1)].rearrange("m j (g c) -> m g j c", g=2),
                               Obank[G % 2][:, 0:2 * HALF].rearrange("m (g j c) -> m g j c", g=2, c=GC),
                               ACT.Copy, scale=alpha[:]).then_inc(o_done, 1)

            sign(0)
            root(0)
            strips(0)
            act.wait_ge(taps_ready, 1)
            relus(0)

            def step(p, more):
                if not isinstance(p, int) or p == 0:
                    act.wait_ge(sel_read, POS + 1)
                patches(p)
                if more:
                    sign(p + 1)
                for G in range(5):
                    gather(p, G)
                if more:
                    root(p + 1)
                    strips(p + 1)
                for G in range(5, 8):
                    gather(p, G)
                if more:
                    relus(p + 1)

            if steps > 0:
                with act.Fori(0, steps) as i:
                    step(i, True)
            step(pairs - 1, False)

        @block.tensor
        def _(pe):
            pe.wait_ge(taps_ready, 1)
            for pos in range(POS):
                if pos >= 4:
                    pe.wait_ge(sel_read, pos - 3)
                pe.matmul(Ybank[(pos % 4) // 2][0:PATCH, pos % 2, :], t_sel16[:, PATCH * pos:PATCH * (pos + 1)],
                          t_w16.rearrange("t l n -> t (l n)"), start=True, stop=True).then_inc(sel_ready, 1)
            for pos in range(POS):
                mm = pe.matmul(Obank[0][0:PATCH, 32 * pos:32 * pos + 32], t_sel16[:, PATCH * pos:PATCH * (pos + 1)],
                               t_b16.rearrange("t l n -> t (l n)"), start=True, stop=True)
                if pos == 0:
                    mm.then_inc(osum_done, 1)
            mm.then_inc(sel_ready, 1)

            def m_free(use):
                if not (isinstance(use, int) and use == 0):
                    pe.wait_ge(m_read, use)

            def stat0(p):
                pe.wait_ge(sum_ready, p + 1)
                m_free(front_use(p, 0))
                pe.matmul(Mbank[0][:, 0:1], gmat[:], col(S_SUM), start=True, stop=True).then_inc(m_ready, 1)

            def conv(p, k):
                use = front_use(p, 1 + k)
                if k == 0:
                    pe.wait_ge(convw_ready, 2)
                    pe.wait_ge(sgn_ready, p + 1)
                m_free(use - 1)
                for tap in range(9):
                    dh, dw = tap // 3, tap % 3
                    mm = pe.matmul(Mbank[(1 + k) % 2][:, 0:CW], convw[:, tap, :],
                                   sgn3[:, CR * k + dh:CR * k + dh + CR, dw:dw + W], start=(tap == 0), stop=(tap == 8))
                mm.then_inc(m_ready, 1)

            def stat(p, n):
                pe.wait_ge(stats_ready, 2 * p + n)
                m_free(front_use(p, CHUNKS + n) - 1)
                pe.matmul(Mbank[(CHUNKS + n) % 2][:, 0:1], gmat[:], mv[:, 0:1] if n == 1 else col(S_T),
                          start=True, stop=True).then_inc(m_ready, 1)

            def reduce(p):
                if not (isinstance(p, int) and p == 0):
                    pe.wait_ge(prod_done, 64 * p)
                pe.wait_ge(high_strip, STRIPS * (p + 1))
                pe.wait_ge(low_strip, STRIPS * (p + 1))
                for dy in range(PY):
                    n = 0
                    for dx in range(PX):
                        for wpart, xpart in ((0, 0), (1, 0), (0, 1)):
                            for b in range(2):
                                px = slice(64 * b, 64 * b + 64)
                                base = (PAD + dy) * IX + PAD + dx
                                rhs = S[px, xpart, :].rearrange("c (s r) -> c s r", r=STRIP)[
                                    :, :, base:base + (PY * (Q * JY - 1)) * IX + 1:PY * IX].rearrange(
                                    "c s (j q) -> c q j s", q=Q)
                                mm = pe.matmul(Ybank[b][:, dy, 0:Q * J],
                                               wred[px, wpart, 112 - 16 * dx:240 - 16 * dx], rhs,
                                               start=(n == 0), stop=(n == 3 * PX - 1))
                                if n == 3 * PX - 1:
                                    mm.then_inc(r_ready, 1)
                            n += 1

            def transposes(p):
                pe.wait_ge(r_done, 4 * (p + 1))
                for n in range(T_ALL):
                    part, q, jy = tplace(n)
                    if n >= 4:
                        on_dve = T_ON_DVE[n - 4]
                        before = DVE_BEFORE[n - 3]
                        if on_dve:
                            pe.wait_ge(t_dve, N_DVE * p + before)
                        else:
                            pe.wait_ge(t_act, N_ACT * p + n - 3 - before)
                    first = PY * (Q * jy + q) * IX
                    for s in range(STRIPS):
                        mm = pe.transpose(tbank(n)[0:PATCH, 128 * s:128 * (s + 1)],
                                          S[:, part, s * STRIP + first:s * STRIP + first + PATCH], ident[:])
                    mm.then_inc(t_ready, 1)
                pe.wait_ge(t_dve, N_DVE * (p + 1))
                pe.wait_ge(t_act, N_ACT * (p + 1))

            def taps(p, g, q):
                u = Q * g + q
                if u >= 2:
                    pe.wait_ge(prod_done, 64 * p + u - 1)
                for dy in range(PY):
                    for n, (wpart, xpart) in enumerate(((0, 0), (1, 0), (0, 1))):
                        rhs = Xv[0:PATCH, xpart, q, :, :].rearrange("k j (b c) -> k b j c", b=2)[
                            :, :, :, GC * g:GC * (g + 1)]
                        mm = pe.matmul(Ybank[u % 2][:, dy, 0:UNIT], Wv[0:PATCH, wpart, g, dy, :], rhs,
                                       start=(n == 0), stop=(n == 2))
                mm.then_inc(y_ready, 1)

            def sums(p, g):
                G = g // 2
                cols = slice(HALF * (g % 2), HALF * (g % 2 + 1))
                pe.wait_ge(prod_done, 64 * p + Q * (g + 1))
                if g % 2 == 0:
                    pe.wait_ge(o_done, 8 * p + max(G, 1))
                for b in range(2):
                    for dy in range(PY):
                        e0 = 24 - 16 * b - 8 * dy
                        for q in range(Q):
                            mm = pe.matmul(Obank[G % 2][32 * q:32 * q + 32, cols], esum[:, e0:e0 + 32],
                                           prod[:, q, UNIT * dy + HALF * b:UNIT * dy + HALF * (b + 1)],
                                           start=(b == 0 and dy == 0), stop=False)
                mm.then_inc(osum_done, 1)
                for b in range(2):
                    for n, (wpart, xpart) in enumerate(((0, 0), (1, 0), (0, 1))):
                        for q in range(Q):
                            mm = pe.matmul(Obank[G % 2][32 * q:32 * q + 32, cols],
                                           wbias[0:PATCH, GROUPS * wpart + g, 16 - 16 * b:48 - 16 * b],
                                           Xv[0:PATCH, xpart, q, :, 64 * b + GC * g:64 * b + GC * (g + 1)],
                                           start=False, stop=(b == 1 and n == 2))
                if g % 2 == 1:
                    mm.then_inc(o_ready, 1)

            def blocks(p, last):
                pe.wait_ge(o_done, 8 * (p + 1) + 1)
                for jy in range(JY):
                    use = back_use(p, jy, last)
                    m_free(use - 1 if jy else use)
                    for s in range(STRIPS):
                        for b in range(2):
                            mm = pe.matmul(Mbank[jy % 2][64 * b:64 * b + 64, 64 * s:64 * s + 64],
                                           osb[:, STRIPS * jy + s, :], back[:, b, :], start=True, stop=True)
                    mm.then_inc(m_ready, 1)

            stat0(0)
            for k in range(CHUNKS):
                conv(0, k)
            stat(0, 1)
            stat(0, 2)
            pe.wait_ge(sel_read, POS + 1)
            reduce(0)

            def step(p, more):
                transposes(p)
                for g in range(GROUPS):
                    taps(p, g, 0)
                    taps(p, g, 1)
                    if g >= 1:
                        sums(p, g - 1)
                    taps(p, g, 2)
                    taps(p, g, 3)
                    if more:
                        if g == 1:
                            stat0(p + 1)
                        for k in CONV_AFTER.get(g, ()):
                            conv(p + 1, k)
                        if g == 8:
                            stat(p + 1, 1)
                        if g == 9:
                            stat(p + 1, 2)
                sums(p, GROUPS - 1)
                if more:
                    reduce(p + 1)
                blocks(p, not more)

            if steps > 0:
                with pe.Fori(0, steps) as i:
                    step(i, True)
            step(pairs - 1, False)

        @block.vector
        def _(dve):
            links = [0]

            def link(ins, base=0):
                links[0] += 1
                ins.then_inc(chain, 1)
                dve.wait_ge(chain, base + links[0])

            def inv_root(y, v, root, u, lk):
                lk(dve.reciprocal(y, root))
                lk(dve.tensor_tensor(u, y, y, ALU.mult))
                lk(dve.tensor_tensor(u, u, v, ALU.mult))
                lk(dve.tensor_scalar(u, u, -0.5, 1.5, ALU.mult, ALU.add))
                lk(dve.tensor_tensor(y, y, u, ALU.mult))

            def max_of(dst, src, width):
                link(dve.tensor_reduce(dst, src, AX.X, ALU.max, apply_absolute_value=True))
                link(dve.tensor_scalar(dst, dst, TINY, None, ALU.max))

            def split(high, low, src):
                link(dve.tensor_copy(high, src))
                link(dve.tensor_tensor(low, src, high, ALU.subtract))

            dve.wait_ge(setup_loaded, LOADS)
            dve.wait_ge(zeroed, ZEROS)
            link(dve.tensor_copy(ident[:], t_id))
            link(dve.tensor_copy(t_sel16, t_sel))
            link(dve.tensor_copy(scale[:], t_par[:, P_SCALE:P_SCALE + 1]))
            sv = t_span[:, 0:GROUPS * O]
            link(dve.tensor_tensor(t_sq, sv, sv, ALU.mult))
            link(dve.tensor_reduce(t_ss, t_sq.rearrange("t (g o) -> t g o", o=O), AX.X, ALU.add))
            vrow = t_par[:, P_ROW:P_ROW + C]
            link(dve.tensor_tensor(t_row, vrow, vrow, ALU.mult))
            link(dve.tensor_reduce(sm[:, 34:35], t_row, AX.X, ALU.add))
            dve.tensor_scalar(sm[:, 35:36], t_par[:, P_VAR:P_VAR + 1], EPS, None, ALU.add).then_inc(setup_sqrt_in, 1)
            max_of(col(40), t_gb, 2 * TAPS * GROUPS)
            link(dve.reciprocal(col(41), col(40)))
            link(dve.tensor_scalar(alpha[:], col(40), 1.0 / (XS * WS), None, ALU.mult))
            max_of(col(42), t_vr, O * C)
            link(dve.reciprocal(col(43), col(42)))
            dve.wait_ge(setup_sqrt_out, 2)
            inv_root(t_rs, t_ss, t_rt, t_u, link)
            inv_root(sm[:, 38:40], sm[:, 34:36], sm[:, 36:38], sm[:, 44:46], link)
            gs, bs = t_span[:, GROUPS * O:GROUPS * (O + 1)], t_span[:, GROUPS * (O + 1):GROUPS * (O + 2)]
            link(dve.tensor_scalar(t_u, gs, sm[0:TAPS, 41:42], WS, ALU.mult, ALU.mult))
            link(dve.tensor_tensor(t_u, t_u, t_rs, ALU.mult))
            link(dve.tensor_tensor(t_w.rearrange("t (g o) -> t g o", o=O), sv.rearrange("t (g o) -> t g o", o=O),
                                   t_u.unsqueeze(2).broadcast_to((TAPS, GROUPS, O)), ALU.mult))
            link(dve.tensor_scalar(t_b, bs, sm[0:TAPS, 41:42], WS, ALU.mult, ALU.mult))
            split(t_w16[:, 0, :], t_w16[:, 1, :], t_w)
            split(t_b16[:, 0, :], t_b16[:, 1, :], t_b)
            link(dve.tensor_scalar(t_vw, t_par[:, P_VT:P_VT + O], col(43), WS, ALU.mult, ALU.mult))
            split(wred[:, 0, 112:128], wred[:, 1, 112:128], t_vw)
            def par(i):
                return t_par[:, i:i + 1]
            link(dve.tensor_tensor(col(46), par(P_GAMMA), col(39), ALU.mult))
            link(dve.tensor_tensor(col(47), par(P_G), col(38), ALU.mult))
            link(dve.tensor_tensor(col(47), col(47), col(46), ALU.mult))
            link(dve.tensor_scalar(red_scale[:], col(47), col(42), 1.0 / (XS * WS), ALU.mult, ALU.mult))
            link(dve.tensor_tensor(col(48), par(P_B), par(P_MEAN), ALU.subtract))
            link(dve.tensor_tensor(col(48), col(48), col(46), ALU.mult))
            link(dve.tensor_tensor(red_bias[:], col(48), par(P_BETA), ALU.add))
            dve.tensor_copy(col(49), col(48)).then_inc(taps_ready, 1)
            for pos in range(POS):
                dy, dx = pos // PX, pos % PX
                dve.wait_ge(sel_ready, pos + 1)
                dve.tensor_copy(
                    Wv[0:PATCH, :, :, dy, O * dx:O * (dx + 1)].rearrange("k l g o -> k (l g) o"),
                    Ybank[(pos % 4) // 2][0:PATCH, pos % 2, :].rearrange("k (n o) -> k n o", o=O)).then_inc(sel_read, 1)
            dve.wait_ge(sel_ready, POS + 1)
            dve.tensor_copy(wbias[0:PATCH, :, 16:32],
                            Obank[0][0:PATCH, :].rearrange("k (p n) -> k n p", n=32)).then_inc(sel_read, 1)
            setup_links = links[0]
            front_links = CHUNKS + 13

            def totals(p):
                dve.wait_ge(x_loaded, 16 * (p + 1))
                dve.tensor_reduce(col(S_SUM), slot(p), AX.X, ALU.add).then_inc(sum_ready, 1)

            def negative_mean(p):
                dve.wait_ge(m_ready, front_use(p, 0) + 1)
                dve.tensor_scalar(col(S_NMEAN), Mbank[0][:, 0:1], -1.0 / HW, None, ALU.mult).then_inc(m_read, 1)
                dve.wait_ge(m_read, front_use(p, 0) + 1)
                dve.tensor_copy(col(12), col(S_NMEAN)).then_inc(nmean_ready, 1)

            def chunk(p, k):
                if k == 0:
                    links[0] = 0
                base = setup_links + front_links * p
                rows = xs[:, bass.ds((p % 2) * HW + CW * k, CW)]
                dve.wait_ge(m_ready, front_use(p, 1 + k) + 1)
                dve.scalar_tensor_tensor(rows, Mbank[(1 + k) % 2][:, 0:CW], scale[:], rows, ALU.mult,
                                         ALU.add).then_inc(m_read, 1)
                written = known(dve, front_use(p, 1 + k) + 1)
                dve.wait_ge(setup_loaded, LOADS)
                dve.wait_ge(m_read, written)
                dve.bn_stats(bn[:, k, :], rows).then_inc(chain, 1)
                links[0] += 1
                counted = known(dve, base + links[0])
                dve.wait_ge(setup_loaded, LOADS)
                dve.wait_ge(chain, counted)
                if k == CHUNKS - 1:
                    dve.bn_aggr(mv[:], bn[:].rearrange("p a b -> p (a b)")).then_inc(stats_ready, 1)

            def spread(p):
                base = setup_links + front_links * p
                dve.wait_ge(m_ready, front_use(p, CHUNKS + 1) + 1)
                link(dve.tensor_copy(col(S_GM), Mbank[(CHUNKS + 1) % 2][:, 0:1]), base)
                link(dve.tensor_tensor(col(S_D), mv[:, 0:1], col(S_GM), ALU.subtract), base)
                link(dve.tensor_tensor(col(S_U), col(S_D), col(S_D), ALU.mult), base)
                dve.tensor_tensor(col(S_T), col(S_U), mv[:, 1:2], ALU.add).then_inc(stats_ready, 1)
                dve.wait_ge(stats_ready, 2 * (p + 1))
                link(dve.tensor_copy(col(13), col(S_T)), base)
                dve.tensor_copy(col(14), col(13)).then_inc(m_read, 1)

            def variance(p):
                base = setup_links + front_links * p
                dve.wait_ge(m_ready, front_use(p, CHUNKS + 2) + 1)
                link(dve.tensor_scalar(col(S_VE), Mbank[(CHUNKS + 2) % 2][:, 0:1], EPS, None, ALU.add), base)
                dve.tensor_copy(col(15), col(S_VE)).then_inc(var_ready, 1)

            def affine(p):
                base = setup_links + front_links * p
                dve.wait_ge(std_ready, p + 1)
                inv_root(col(S_Y), col(S_VE), col(S_SD), col(S_U), lambda ins: link(ins, base))
                link(dve.tensor_scalar(col(S_RS), col(S_Y), XS, None, ALU.mult), base)
                link(dve.tensor_tensor(col(16), col(S_GM), col(S_RS), ALU.mult), base)
                link(dve.tensor_scalar(col(S_NB), col(16), -1.0, None, ALU.mult), base)
                dve.tensor_copy(col(17), col(S_NB)).then_inc(affine_ready, 1)
                dve.tensor_copy(col(18), col(S_NB)).then_inc(m_read, 1)
                assert links[0] == front_links, links[0]

            def patches(p):
                for n in range(T_ALL):
                    if T_ON_DVE[n]:
                        part, q, jy = tplace(n)
                        dve.wait_ge(t_ready, T_ALL * p + n + 1)
                        dve.tensor_copy(patch_rows(part, q, jy).bitcast(U32),
                                        tbank(n)[0:PATCH, :].bitcast(U32)).then_inc(t_dve, 1)

            def product(p, g, q):
                u = Q * g + q
                dve.wait_ge(y_ready, 64 * p + u + 1)
                if q == 0:
                    if u == 0:
                        dve.wait_ge(r_done, 4 * (p + 1))
                    dve.wait_ge(osum_done, GROUPS * p + g + 1)
                dve.tensor_tensor(
                    prod[:, q, :].rearrange("m (d n c) -> m d n c", d=PY, c=GC),
                    Ybank[u % 2][:, :, 0:UNIT].rearrange("m d (n c) -> m d n c", c=GC),
                    R[:, :, q, :, :].rearrange("m d b j -> m d (b j)").unsqueeze(3).broadcast_to((128, PY, 2 * J, GC)),
                    ALU.mult).then_inc(prod_done, 1)

            def outputs(p, last):
                for jy in range(JY):
                    use = back_use(p, jy, last)
                    rows = xs[:, bass.ds((p % 2) * HW + CW * jy, CW)].rearrange(
                        "p (y s x) -> p s y x", y=8, s=STRIPS)
                    dve.wait_ge(m_ready, use + 1)
                    dve.tensor_tensor(rows, Mbank[jy % 2][:, 0:CW].rearrange("p (s y x) -> p s y x", s=STRIPS, y=8),
                                      rows, ALU.add).then_inc(m_read, 1)
                dve.wait_ge(m_read, back_use(p, JY - 1, last) + 1)
                dve.tensor_copy(col(19), col(S_NB)).then_inc(out_added, 1)

            totals(0)
            negative_mean(0)
            for k in range(CHUNKS):
                chunk(0, k)
            spread(0)
            variance(0)
            affine(0)

            def step(p, more):
                patches(p)
                for g in range(GROUPS):
                    for q in range(Q):
                        product(p, g, q)
                        if more:
                            if (g, q) == (0, 3):
                                totals(p + 1)
                            if (g, q) == (2, 0):
                                negative_mean(p + 1)
                            if q == 1:
                                for k in CONV_AFTER.get(g - 1, ()):
                                    chunk(p + 1, k)
                            if (g, q) == (9, 1):
                                spread(p + 1)
                            if (g, q) == (10, 1):
                                variance(p + 1)
                            if (g, q) == (10, 3):
                                affine(p + 1)
                outputs(p, not more)

            if steps > 0:
                with dve.Fori(0, steps) as i:
                    step(i, True)
            step(pairs - 1, False)


def constants():
    import numpy as np

    c = np.zeros((128, C_N), np.float32)
    c[:, C_ID:C_ID + 128] = np.eye(128)
    for dy in range(PY):
        for dx in range(PX):
            for ky in range(K):
                for kx in range(K):
                    c[ky * K + kx, C_SEL + (dy * PX + dx) * PATCH + (dy + ky) * IX + dx + kx] = 1
    for m in range(128):
        c[m, C_G + m // 2 * 2:C_G + m // 2 * 2 + 2] = 0.5
        c[m, C_E + 24 + m // O] = 1
    for q in range(Q):
        for b in range(2):
            for dy in range(PY):
                for dx in range(PX):
                    c[32 * q + 16 * b + PX * dy + dx, C_R + 64 * b + 8 * (PY * q + dy) + dx] = 1
    return c


def layouts(w, scale, v_reduce, per_o, v_span, g_span, b_span):
    import numpy as np

    p = np.zeros((128, P_N), np.float32)
    p[:, P_SCALE] = np.tile(scale, 2)
    for i, v in enumerate(per_o):
        p[:, P_G + i] = np.tile(v, PX)
    p[:, P_VT:P_VT + O] = np.tile(v_reduce.T, (2, 1))
    p[:, P_ROW:P_ROW + C] = np.tile(v_reduce, (PX, 1))
    p[:, P_CONV:P_N] = np.tile(w.transpose(1, 2, 3, 0).reshape(C, 9 * C), (2, 1))
    span = np.concatenate([v_span.reshape(TAPS, GROUPS * O), g_span.reshape(TAPS, GROUPS),
                           b_span.reshape(TAPS, GROUPS)], axis=1)
    gb = np.concatenate([g_span, b_span]).reshape(1, -1)
    return p, np.ascontiguousarray(span), gb, np.ascontiguousarray(v_reduce.reshape(1, -1))


def inputs_of(x, L0_conv_weight, L0_conv_scale, L1_conv_v_reduce, L1_conv_g_reduce, L1_conv_b_reduce,
              L1_conv_bn_gamma, L1_conv_bn_beta, L1_conv_bn_mean, L1_conv_bn_var, L1_conv_v_span,
              L1_conv_g_span, L1_conv_b_span):
    import numpy as np

    per_o = [np.asarray(a) for a in (L1_conv_g_reduce, L1_conv_b_reduce, L1_conv_bn_gamma, L1_conv_bn_beta,
                                     L1_conv_bn_mean, L1_conv_bn_var)]
    p, span, gb, vr = layouts(np.asarray(L0_conv_weight), np.asarray(L0_conv_scale), np.asarray(L1_conv_v_reduce),
                              per_o, np.asarray(L1_conv_v_span), np.asarray(L1_conv_g_span),
                              np.asarray(L1_conv_b_span))
    return {"x_dram": np.ascontiguousarray(x), "consts_dram": constants(), "params_dram": p, "span_dram": span,
            "gb_dram": gb, "vr_dram": vr}


def kernel(**inputs):
    import concourse.bacc as bacc
    from concourse.bass_utils import run_bass_kernel_spmd

    arrays = inputs_of(**inputs)
    nc = bacc.Bacc("TRN2", target_bir_lowering=False, num_devices=1)
    ins = [nc.dram_tensor(n, a.shape, mybir.dt.from_np(a.dtype), kind="ExternalInput").ap() for n, a in arrays.items()]
    out = nc.dram_tensor("out_dram", (B, C, H, W), F32, kind="ExternalOutput").ap()
    build(nc, *ins, out)
    r = run_bass_kernel_spmd(nc, [arrays], core_ids=[0])
    return r.results[0]["out_dram"]
```

```python
from contextlib import ExitStack

import concourse.bass as bass
from concourse import mybir

F32 = mybir.dt.float32
F16 = mybir.dt.float16
BF16 = mybir.dt.bfloat16
U32 = mybir.dt.uint32
ALU = mybir.AluOpType
ACT = mybir.ActivationFunctionType
AX = mybir.AxisListType

B, C, H, W = 32, 64, 56, 56
PAIRS = B // 2
HW = H * W
GROUPS, GC = 16, 4
O = 16
K, PAD = 7, 3
TAPS = K * K
PY, PX = 2, 8
POS = PY * PX
IY, IX = PY + K - 1, PX + K - 1
PATCH = IY * IX
STRIPS = W // PX
ROWS = H + 2 * PAD
STRIP = ROWS * IX
Q = 4
JY = H // (PY * Q)
J = JY * STRIPS
UNIT = 2 * J * GC
HALF = J * GC
CR = 8
CHUNKS = H // CR
CW = CR * W
XS, WS = 256.0, 1024.0
EPS = 1e-5
TINY = 1e-30

C_ID, C_SEL = 0, 128
C_G = C_SEL + POS * PATCH
C_E = C_G + 128
C_R = C_E + 56
C_M = C_R + 128
C_N = C_M + 2
P_SCALE, P_G, P_B, P_GAMMA, P_BETA, P_MEAN, P_VAR, P_VT = range(8)
P_ROW = P_VT + O
P_CONV = P_ROW + C
P_N = P_CONV + 9 * C

FIRST_LOADS, LOADS, ZEROS = 16 * 2, 16 * 8, 4
XLOAD = 16 * 4
FRONT_M, BACK_M = CHUNKS + 3, 8
T_ALL = 2 * Q * STRIPS
BACK_AFTER = {0: 2, 1: 5, 2: 8, 3: 11, 4: 14, 5: 17, 6: 20, 7: 23}
T_ON_DVE = [n % 5 in (1, 4) if n < 26 else n % 9 not in (0, 2, 4, 6) for n in range(T_ALL)]
CONV_AT = {3 + k: k for k in range(CHUNKS)}


def build(nc, x, consts, params, span, gb_all, vr_all, out, pairs=PAIRS):
    xv = x.rearrange("(p b) (gh gp c) h w -> p gp b gh c (h w)", b=2, gp=2, c=GC)
    ov = out.rearrange("(p b) (gh gp c) h w -> p gp b gh c (h w)", b=2, gp=2, c=GC)

    with ExitStack() as ctx:
        def sb(name, shape, dt=F32):
            return ctx.enter_context(nc.sbuf_tensor(name, shape, dt))

        def sem(name):
            return ctx.enter_context(nc.semaphore(name))

        X = sb("patches", [128, 2 * Q * J * 128], F16)
        wspan = sb("wspan", [128, 2 * GROUPS * PY * 128], F16)
        wbias = sb("wbias", [128, 2 * GROUPS * 32 + 16], F16)
        S = sb("strips", [128, 2, STRIPS * STRIP], F16)
        xs = sb("xs", [128, 2 * HW])
        xn = sb("xn", [128, 2, H * IX])
        R = sb("relu", [128, PY, Q, 2, J])
        prod = sb("prod", [128, Q + 1, PY * UNIT])
        osb = sb("osb", [128, J, C])
        ident = sb("ident", [128, 128], F16)
        gmat = sb("gmat", [128, 128])
        esum = sb("esum", [128, 56])
        back = sb("back", [128, 128])
        convw = sb("convw", [128, 9, 128], BF16)
        wred = sb("wred", [128, 2, 2, 48], F16)
        scale = sb("scale", [128, 1])
        red_scale = sb("red_scale", [128, 1])
        red_bias = sb("red_bias", [128, 1])
        alpha = sb("alpha", [128, 1])
        sm = sb("small", [128, 64])
        bn = sb("bn", [128, CHUNKS, 6])
        mv = sb("mv", [128, 2])
        sgn = S[:, 1, 0:(H + 2) * (W + 2)].bitcast(BF16)
        sgn3 = sgn.rearrange("p (h w) -> p h w", w=W + 2)

        Ybank = [ctx.enter_context(nc.psum_tensor(f"ybank{i}", [128, PY, 512], F32)) for i in range(2)]
        Obank = [ctx.enter_context(nc.psum_tensor(f"obank{i}", [128, 512], F32)) for i in range(2)]
        Mbank = [ctx.enter_context(nc.psum_tensor(f"mbank{i}", [128, 512], F32)) for i in range(2)]

        Xv = X[:].rearrange("k (l q j p) -> k l q j p", l=2, q=Q, p=128)
        Wv = wspan[:].rearrange("k (l g d m) -> k l g d m", l=2, g=GROUPS, d=PY)

        first_loaded = sem("first_loaded")
        setup_loaded = sem("setup_loaded")
        zeroed = sem("zeroed")
        setup_sqrt_in = sem("setup_sqrt_in")
        setup_sqrt_out = sem("setup_sqrt_out")
        convw_ready = sem("convw_ready")
        taps_ready = sem("taps_ready")
        sel_ready = sem("sel_ready")
        sel_read = sem("sel_read")
        chain = sem("chain")
        x_loaded = sem("x_loaded")
        stored = sem("stored")
        sum_ready = sem("sum_ready")
        m_ready = sem("m_ready")
        m_read = sem("m_read")
        nmean_ready = sem("nmean_ready")
        sgn_zeroed = sem("sgn_zeroed")
        sgn_ready = sem("sgn_ready")
        stats_ready = sem("stats_ready")
        var_ready = sem("var_ready")
        std_ready = sem("std_ready")
        affine_ready = sem("affine_ready")
        low_zeroed = sem("low_zeroed")
        high_strip = sem("high_strip")
        low_strip = sem("low_strip")
        r_ready = sem("r_ready")
        r_done = sem("r_done")
        t_ready = sem("t_ready")
        t_act = sem("t_act")
        t_dve = sem("t_dve")
        y_ready = sem("y_ready")
        prod_done = sem("prod_done")
        osum_done = sem("osum_done")
        o_ready = sem("o_ready")
        o_done = sem("o_done")
        out_added = sem("out_added")

        def slot(p, places=slice(0, 128)):
            return xs[places, bass.ds((p % 2) * HW, HW)]

        def front_use(p, k):
            if isinstance(p, int):
                return k if p == 0 else FRONT_M + (FRONT_M + BACK_M) * (p - 1) + k
            return (p - 1) * (FRONT_M + BACK_M) + FRONT_M + k

        def back_use(p, k, last):
            return p * (FRONT_M + BACK_M) + (FRONT_M if last else 2 * FRONT_M) + k

        def known(eng, value):
            return value if isinstance(value, int) else eng.to_reg(value)

        def place(g, q):
            return Q if q == 0 and g % 2 else q

        def tbank(n):
            return Ybank[n % 2][:, n % 4 // 2, 0:STRIPS * 64].bitcast(F16)

        def tplace(n):
            return n // STRIPS % 2, n // (2 * STRIPS), n % STRIPS

        def strip_range(s):
            return (PAD if s == 0 else 0), (IX - PAD if s == STRIPS - 1 else IX)

        def strip(part, s):
            return S[:, part, s * STRIP + PAD * IX:s * STRIP + (PAD + H) * IX].rearrange("p (h w) -> p h w", w=IX)

        def xn3(s):
            return xn[:, s % 2, :].rearrange("p (h w) -> p h w", w=IX)

        def patch_rows(part, q, s):
            return Xv[0:PATCH, part, q, JY * s:JY * (s + 1), :].rearrange("k j p -> k (j p)")

        def bplace(n):
            return (range(2 * (n // 2), min(2 * (n // 2) + 2, JY)), range(4) if n % 2 == 0 else range(4, STRIPS))

        def bbank(n):
            return (Mbank + Obank)[n % 4]

        DVE_BEFORE = [sum(T_ON_DVE[:n]) for n in range(T_ALL + 1)]
        N_DVE, N_ACT = DVE_BEFORE[T_ALL], T_ALL - DVE_BEFORE[T_ALL]

        tmp = X[:].bitcast(F32)
        t_id, t_sel = tmp[:, 0:128], tmp[0:TAPS, 128:128 + POS * PATCH]
        t_span = tmp[0:TAPS, 2048:2048 + GROUPS * (O + 2)]
        t_gb = tmp[:, 2560:2560 + 2 * TAPS * GROUPS]
        t_vr = tmp[:, 4224:4224 + O * C]
        t_par = tmp[:, 5376:5376 + P_N]
        t_sq = tmp[0:TAPS, 6272:6528]
        t_ss = tmp[0:TAPS, 6528:6544]
        t_rt = tmp[0:TAPS, 6560:6576]
        t_rs = tmp[0:TAPS, 6592:6608]
        t_u = tmp[0:TAPS, 6624:6640]
        t_w = tmp[0:TAPS, 6656:6912]
        t_b = tmp[0:TAPS, 6912:6928]
        t_mask = tmp[:, 5354:5356]
        t_row = tmp[:, 6944:7008]
        t_vw = tmp[:, 7040:7056]
        t_mw = tmp[:, 7072:7088]
        t_sel16 = X[0:TAPS, 16384:16384 + POS * PATCH]
        t_w16 = X[0:TAPS, 18432:18432 + 512].rearrange("t (l n) -> t l n", l=2)
        t_b16 = X[0:TAPS, 19200:19232].rearrange("t (l n) -> t l n", l=2)

        def col(i):
            return sm[:, i:i + 1]
        (S_SUM, S_NMEAN, S_GM, S_D, S_T, S_VE, S_SD, S_Y, S_U, S_RS, S_NB) = range(11)

        block = ctx.enter_context(nc.Block())

        @block.sync
        def _(sp):
            def load(p, into):
                for gp in range(2):
                    for b in range(2):
                        sp.dma_start(into[64 * gp + 32 * b:64 * gp + 32 * b + 32], xv[p][gp][b]).then_inc(x_loaded, 16)

            sp.dma_start(gmat[:], consts[:, C_G:C_E]).then_inc(first_loaded, 16)
            sp.dma_start(t_par, params).then_inc(first_loaded, 16)
            load(0, xs[:, 0:HW])
            for dst, src in ((t_id, consts[:, C_ID:C_ID + 128]), (t_sel, consts[0:TAPS, C_SEL:C_G]),
                             (esum[:], consts[:, C_E:C_R]), (back[:], consts[:, C_R:C_M]), (t_mask, consts[:, C_M:C_N]),
                             (t_span, span), (t_gb, gb_all.broadcast_to((128, 2 * TAPS * GROUPS))),
                             (t_vr, vr_all.broadcast_to((128, O * C)))):
                sp.dma_start(dst, src).then_inc(setup_loaded, 16)
            sp.wait_ge(x_loaded, XLOAD)
            load(1, xs[:, HW:2 * HW])

            def step(p, load_next):
                sp.wait_ge(out_added, p + 1)
                for gp in range(2):
                    for b in range(2):
                        quarter = slice(64 * gp + 32 * b, 64 * gp + 32 * b + 32)
                        sp.dma_start(ov[p][gp][b], slot(p, quarter)).then_inc(stored, 16)
                sp.wait_ge(stored, XLOAD * (p + 1))
                if load_next:
                    sp.wait_ge(x_loaded, XLOAD * (p + 2))
                    for gp in range(2):
                        for b in range(2):
                            quarter = slice(64 * gp + 32 * b, 64 * gp + 32 * b + 32)
                            sp.dma_start(slot(p, quarter), xv[p + 2][gp][b]).then_inc(x_loaded, 16)

            if pairs > 2:
                with sp.Fori(0, pairs - 2) as p:
                    step(p, True)
            step(pairs - 2, False)
            step(pairs - 1, False)

        @block.gpsimd
        def _(pool):
            pool.memset(S[:].rearrange("p l n -> p (l n)").bitcast(U32), 0).then_inc(zeroed, 1)
            pool.memset(wbias[:].bitcast(U32), 0).then_inc(zeroed, 1)
            pool.memset(wred[:].rearrange("p a b c -> p (a b c)").bitcast(U32), 0).then_inc(zeroed, 1)
            pool.memset(convw[:].rearrange("p a b -> p (a b)").bitcast(U32), 0).then_inc(zeroed, 1)
            pool.wait_ge(zeroed, ZEROS)

            def front(p):
                transposed = known(pool, T_ALL * p)
                pool.wait_ge(zeroed, ZEROS)
                if not (isinstance(p, int) and p == 0):
                    pool.wait_ge(t_ready, transposed)
                pool.memset(sgn.bitcast(U32), 0).then_inc(sgn_zeroed, 1)
                convolved = known(pool, front_use(p, CHUNKS) + 1)
                pool.wait_ge(zeroed, ZEROS)
                pool.wait_ge(m_ready, convolved)
                pool.memset(S[:, 1, :].bitcast(U32), 0).then_inc(low_zeroed, 1)
                pool.wait_ge(low_zeroed, p + 1)
                for s in range(STRIPS):
                    lo, hi = strip_range(s)
                    pool.wait_ge(high_strip, STRIPS * p + s + 1)
                    pool.tensor_tensor(strip(1, s)[:, :, lo:hi], xn3(s)[:, :, lo:hi], strip(0, s)[:, :, lo:hi],
                                       ALU.subtract).then_inc(low_strip, 1)

            front(0)
            with pool.Fori(1, pairs) as p:
                front(p)

        @block.scalar
        def _(act):
            act.wait_ge(first_loaded, FIRST_LOADS)
            act.wait_ge(zeroed, ZEROS)
            for place_in in range(0, 128, 32):
                image = place_in // 32 % 2
                for gp in range(2):
                    act.activation(convw[place_in:place_in + 32, :, 64 * gp + 32 * image:64 * gp + 32 * image + 32],
                                   t_par[place_in:place_in + 32, P_CONV:P_N].rearrange(
                                       "p (t o) -> p t o", t=9)[:, :, 32 * gp:32 * gp + 32],
                                   ACT.Sign).then_inc(convw_ready, 1)

            def setup_roots():
                act.wait_ge(setup_sqrt_in, 1)
                act.activation(t_rt, t_ss, ACT.Sqrt).then_inc(setup_sqrt_out, 1)
                act.activation(sm[:, 36:38], sm[:, 34:36], ACT.Sqrt).then_inc(setup_sqrt_out, 1)
                act.wait_ge(setup_sqrt_out, 2)
                act.activation(sm[:, 50:51], sm[:, 36:37], ACT.Copy).then_inc(o_done, 1)

            def sign(p):
                turn = known(act, p + 1)
                act.wait_ge(first_loaded, FIRST_LOADS)
                act.wait_ge(nmean_ready, turn)
                act.wait_ge(sgn_zeroed, turn)
                act.activation(sgn3[:, 1:H + 1, 1:W + 1], slot(p).rearrange("p (h w) -> p h w", w=W),
                               ACT.Sign, bias=col(S_NMEAN)).then_inc(sgn_ready, 1)

            def root(p):
                act.wait_ge(var_ready, p + 1)
                act.activation(col(S_SD), col(S_VE), ACT.Sqrt).then_inc(std_ready, 1)

            def strips(p):
                act.wait_ge(affine_ready, p + 1)
                if not (isinstance(p, int) and p == 0):
                    act.wait_ge(t_ready, T_ALL * p)
                x3 = slot(p).rearrange("p (h w) -> p h w", w=W)
                for s in range(STRIPS):
                    lo, hi = strip_range(s)
                    src = x3[:, :, PX * s - PAD + lo:PX * s - PAD + hi]
                    read = known(act, STRIPS * p + max(s - 1, 0))
                    act.wait_ge(zeroed, ZEROS)
                    if not (isinstance(read, int) and read == 0):
                        act.wait_ge(low_strip, read)
                    act.activation(xn3(s)[:, :, lo:hi], src, ACT.Identity, bias=col(S_NB), scale=col(S_RS))
                    act.activation(strip(0, s)[:, :, lo:hi], src, ACT.Identity, bias=col(S_NB),
                                   scale=col(S_RS)).then_inc(high_strip, 1)

            def relus(p):
                for dy in range(PY):
                    for b in range(2):
                        act.wait_ge(r_ready, 4 * p + 2 * dy + b + 1)
                        act.activation(R[:, dy, :, b, :],
                                       Ybank[b][:, dy, 0:Q * J].rearrange("m (q j) -> m q j", q=Q),
                                       ACT.Relu, bias=red_bias[:], scale=red_scale[:]).then_inc(r_done, 1)

            def patches(p):
                for n in range(T_ALL):
                    if not T_ON_DVE[n]:
                        part, q, s = tplace(n)
                        act.wait_ge(t_ready, T_ALL * p + n + 1)
                        act.activation(patch_rows(part, q, s), tbank(n)[0:PATCH, :], ACT.Copy).then_inc(t_act, 1)

            def gather(p, G):
                if G == 0:
                    act.wait_ge(m_ready, FRONT_M + (FRONT_M + BACK_M) * p)
                act.wait_ge(o_ready, 8 * p + G + 1)
                act.activation(osb[:].rearrange("m j (b g c) -> m b j g c", b=2, c=GC)[:, :, :, G, :],
                               Obank[G % 2][:, 0:UNIT].rearrange("m (b j c) -> m b j c", b=2, c=GC),
                               ACT.Copy, scale=alpha[:]).then_inc(o_done, 1)

            sign(0)
            setup_roots()
            root(0)
            strips(0)
            act.wait_ge(taps_ready, 1)
            relus(0)
            act.wait_ge(sel_read, POS + 1)

            def step(p, more):
                patches(p)
                if more:
                    sign(p + 1)
                for G in range(5):
                    gather(p, G)
                if more:
                    root(p + 1)
                    strips(p + 1)
                for G in range(5, 8):
                    gather(p, G)
                if more:
                    relus(p + 1)

            with act.Fori(0, pairs - 1) as p:
                step(p, True)
            step(pairs - 1, False)

        @block.tensor
        def _(pe):
            def select():
                pe.wait_ge(taps_ready, 1)
                for pos in range(POS):
                    if pos >= 4:
                        pe.wait_ge(sel_read, pos - 3)
                    pe.matmul(Ybank[(pos % 4) // 2][0:PATCH, pos % 2, :], t_sel16[:, PATCH * pos:PATCH * (pos + 1)],
                              t_w16.rearrange("t l n -> t (l n)"), start=True, stop=True).then_inc(sel_ready, 1)
                for pos in range(POS):
                    mm = pe.matmul(Obank[0][0:PATCH, 32 * pos:32 * pos + 32],
                                   t_sel16[:, PATCH * pos:PATCH * (pos + 1)],
                                   t_b16.rearrange("t l n -> t (l n)"), start=True, stop=True)
                    if pos < 2:
                        mm.then_inc(osum_done, 1)
                mm.then_inc(sel_ready, 1)

            def m_free(use):
                if not (isinstance(use, int) and use == 0):
                    pe.wait_ge(m_read, use)

            def stat0(p):
                if isinstance(p, int) and p == 0:
                    pe.wait_ge(first_loaded, FIRST_LOADS)
                pe.wait_ge(sum_ready, p + 1)
                m_free(front_use(p, 0))
                pe.matmul(Mbank[0][:, 0:1], gmat[:], col(S_SUM), start=True, stop=True).then_inc(m_ready, 1)

            def conv(p, k):
                use = front_use(p, 1 + k)
                if k == 0:
                    pe.wait_ge(convw_ready, 8)
                    pe.wait_ge(sgn_ready, p + 1)
                m_free(use - 1)
                for tap in range(9):
                    dh, dw = tap // 3, tap % 3
                    mm = pe.matmul(Mbank[(1 + k) % 2][:, 0:CW], convw[:, tap, :],
                                   sgn3[:, CR * k + dh:CR * k + dh + CR, dw:dw + W], start=(tap == 0), stop=(tap == 8))
                mm.then_inc(m_ready, 1)

            def stat(p, n):
                pe.wait_ge(stats_ready, 2 * p + n)
                m_free(front_use(p, CHUNKS + n) - 1)
                pe.matmul(Mbank[(CHUNKS + n) % 2][:, 0:1], gmat[:], mv[:, 0:1] if n == 1 else col(S_T),
                          start=True, stop=True).then_inc(m_ready, 1)

            def reduce(p):
                if not (isinstance(p, int) and p == 0):
                    pe.wait_ge(prod_done, 64 * p)
                pe.wait_ge(high_strip, STRIPS * (p + 1))
                pe.wait_ge(low_strip, STRIPS * (p + 1))
                for dy in range(PY):
                    for b in range(2):
                        n = 0
                        for odd in range(2):
                            for wpart, xpart in ((0, 0), (1, 0), (0, 1)):
                                for t in range(4):
                                    base = (PAD + dy) * IX + PAD + 2 * t + odd
                                    rhs = S[:, xpart, :].rearrange("c (s r) -> c s r", r=STRIP)[
                                        :, :, base:base + (PY * (Q * JY - 1)) * IX + 1:PY * IX].rearrange(
                                        "c s (j q) -> c q s j", q=Q)
                                    mm = pe.matmul(Ybank[b][32 * t:32 * t + 32, dy, 0:Q * J],
                                                   wred[:, b, wpart, 16 - 16 * odd:48 - 16 * odd], rhs,
                                                   start=(n == 0), stop=(n == 5))
                                n += 1
                        mm.then_inc(r_ready, 1)

            def transposes(p, behind):
                for n in range(T_ALL):
                    if behind:
                        for k in [k for k, after in BACK_AFTER.items() if after == n]:
                            block(p - 1, k, False)
                    if n < 4:
                        pe.wait_ge(r_done, 4 * p + n + 1)
                    part, q, s = tplace(n)
                    if n >= 4:
                        on_dve = T_ON_DVE[n - 4]
                        before = DVE_BEFORE[n - 3]
                        if on_dve:
                            pe.wait_ge(t_dve, N_DVE * p + before)
                        else:
                            pe.wait_ge(t_act, N_ACT * p + n - 3 - before)
                    for jy in range(JY):
                        first = s * STRIP + PY * (Q * jy + q) * IX
                        mm = pe.transpose(tbank(n)[0:PATCH, 128 * jy:128 * (jy + 1)],
                                          S[:, part, first:first + PATCH], ident[:])
                    mm.then_inc(t_ready, 1)

            def of_group(xpart, q, g):
                return Xv[0:PATCH, xpart, q, :, :].rearrange("k j (gp b g c) -> k gp g b j c", gp=2, b=2, c=GC)[
                    :, g % 2, g // 2]

            def taps(p, g, q):
                u = Q * g + q
                if u >= 2:
                    pe.wait_ge(prod_done, 64 * p + u - 1)
                else:
                    done = T_ALL - 1 + u
                    pe.wait_ge(t_dve, N_DVE * p + DVE_BEFORE[done])
                    pe.wait_ge(t_act, N_ACT * p + done - DVE_BEFORE[done])
                for dy in range(PY):
                    for n, (wpart, xpart) in enumerate(((0, 0), (1, 0), (0, 1))):
                        mm = pe.matmul(Ybank[u % 2][:, dy, 0:UNIT], Wv[0:PATCH, wpart, g, dy, :], of_group(xpart, q, g),
                                       start=(n == 0), stop=(n == 2))
                mm.then_inc(y_ready, 1)

            def sums(p, g):
                G, gp = g // 2, g % 2
                pe.wait_ge(prod_done, 64 * p + Q * (g + 1))
                if g % 2 == 0:
                    pe.wait_ge(o_done, 8 * p + max(G, 1))
                    if G == 0:
                        pe.wait_ge(m_read, FRONT_M + (FRONT_M + BACK_M) * p)
                for dy in range(PY):
                    e0 = 24 - 16 * gp - 8 * dy
                    for q in range(Q):
                        mm = pe.matmul(Obank[G % 2][32 * q:32 * q + 32, 0:UNIT], esum[:, e0:e0 + 32],
                                       prod[:, place(g, q), UNIT * dy:UNIT * (dy + 1)],
                                       start=(gp == 0 and dy == 0), stop=False)
                mm.then_inc(osum_done, 1)
                for n, (wpart, xpart) in enumerate(((0, 0), (1, 0), (0, 1))):
                    w0 = 32 * (GROUPS * wpart + g) + 16 - 16 * gp
                    for q in range(Q):
                        mm = pe.matmul(Obank[G % 2][32 * q:32 * q + 32, 0:UNIT], wbias[0:PATCH, w0:w0 + 32],
                                       of_group(xpart, q, g), start=False, stop=(gp == 1 and n == 2))
                if g % 2 == 1:
                    mm.then_inc(o_ready, 1)

            def block(p, n, last):
                read = known(pe, back_use(p, max(n - 3, 0), last))
                gathered = known(pe, 8 * (p + 1) + 1)
                pe.wait_ge(sel_read, POS + 1)
                if n == 0:
                    pe.wait_ge(o_done, gathered)
                pe.wait_ge(m_read, read)
                jys, strips = bplace(n)
                for i, st in enumerate(strips):
                    mm = pe.transpose(bbank(n)[0:64 * len(jys), 128 * i:128 * (i + 1)],
                                      osb[:, JY * st + jys[0]:JY * st + jys[0] + len(jys), :].rearrange(
                                          "m j c -> m (j c)"), back[:])
                mm.then_inc(m_ready, 1)

            stat0(0)
            for k in range(CHUNKS):
                conv(0, k)
            stat(0, 1)
            stat(0, 2)
            select()
            pe.wait_ge(sel_read, POS + 1)
            reduce(0)

            def step(p, more, behind):
                transposes(p, behind)
                for g in range(GROUPS):
                    taps(p, g, 0)
                    taps(p, g, 1)
                    if g >= 1:
                        sums(p, g - 1)
                    if more:
                        if g == 1:
                            stat0(p + 1)
                        if g in CONV_AT:
                            conv(p + 1, CONV_AT[g])
                        if g == 10:
                            stat(p + 1, 1)
                        if g == 11:
                            stat(p + 1, 2)
                    taps(p, g, 2)
                    taps(p, g, 3)
                sums(p, GROUPS - 1)
                if more:
                    reduce(p + 1)

            step(0, True, False)
            if pairs > 2:
                with pe.Fori(1, pairs - 1) as p:
                    step(p, True, True)
            step(pairs - 1, False, True)
            for n in range(BACK_M):
                block(pairs - 1, n, True)

        @block.vector
        def _(dve):
            links = [0]

            def link(ins, base=0):
                links[0] += 1
                ins.then_inc(chain, 1)
                dve.wait_ge(chain, base + links[0])

            def inv_root(y, v, root, u, lk):
                lk(dve.reciprocal(y, root))
                lk(dve.tensor_tensor(u, y, y, ALU.mult))
                lk(dve.tensor_tensor(u, u, v, ALU.mult))
                lk(dve.tensor_scalar(u, u, -0.5, 1.5, ALU.mult, ALU.add))
                lk(dve.tensor_tensor(y, y, u, ALU.mult))

            def max_of(dst, src, width):
                link(dve.tensor_reduce(dst, src, AX.X, ALU.max, apply_absolute_value=True))
                link(dve.tensor_scalar(dst, dst, TINY, None, ALU.max))

            def split(high, low, src):
                link(dve.tensor_copy(high, src))
                link(dve.tensor_tensor(low, src, high, ALU.subtract))

            sv = t_span[:, 0:GROUPS * O]

            def squares():
                dve.wait_ge(first_loaded, FIRST_LOADS)
                dve.wait_ge(setup_loaded, LOADS)
                link(dve.tensor_copy(scale[:], t_par[:, P_SCALE:P_SCALE + 1]))
                link(dve.tensor_tensor(t_sq, sv, sv, ALU.mult))
                link(dve.tensor_reduce(t_ss, t_sq.rearrange("t (g o) -> t g o", o=O), AX.X, ALU.add))
                vrow = t_par[:, P_ROW:P_ROW + C]
                link(dve.tensor_tensor(t_row, vrow, vrow, ALU.mult))
                link(dve.tensor_reduce(sm[:, 34:35], t_row, AX.X, ALU.add))
                dve.tensor_scalar(sm[:, 35:36], t_par[:, P_VAR:P_VAR + 1], EPS, None, ALU.add).then_inc(setup_sqrt_in, 1)

            def setup():
                dve.wait_ge(zeroed, ZEROS)
                link(dve.tensor_copy(ident[:], t_id))
                link(dve.tensor_copy(t_sel16, t_sel))
                max_of(col(40), t_gb, 2 * TAPS * GROUPS)
                link(dve.reciprocal(col(41), col(40)))
                link(dve.tensor_scalar(alpha[:], col(40), 1.0 / (XS * WS), None, ALU.mult))
                max_of(col(42), t_vr, O * C)
                link(dve.reciprocal(col(43), col(42)))
                dve.wait_ge(setup_sqrt_out, 2)
                inv_root(t_rs, t_ss, t_rt, t_u, link)
                inv_root(sm[:, 38:40], sm[:, 34:36], sm[:, 36:38], sm[:, 44:46], link)
                gs, bs = t_span[:, GROUPS * O:GROUPS * (O + 1)], t_span[:, GROUPS * (O + 1):GROUPS * (O + 2)]
                link(dve.tensor_scalar(t_u, gs, sm[0:TAPS, 41:42], WS, ALU.mult, ALU.mult))
                link(dve.tensor_tensor(t_u, t_u, t_rs, ALU.mult))
                link(dve.tensor_tensor(t_w.rearrange("t (g o) -> t g o", o=O), sv.rearrange("t (g o) -> t g o", o=O),
                                       t_u.unsqueeze(2).broadcast_to((TAPS, GROUPS, O)), ALU.mult))
                link(dve.tensor_scalar(t_b, bs, sm[0:TAPS, 41:42], WS, ALU.mult, ALU.mult))
                split(t_w16[:, 0, :], t_w16[:, 1, :], t_w)
                split(t_b16[:, 0, :], t_b16[:, 1, :], t_b)
                link(dve.tensor_scalar(t_vw, t_par[:, P_VT:P_VT + O], col(43), WS, ALU.mult, ALU.mult))
                for b in range(2):
                    link(dve.tensor_scalar(t_mw, t_vw, t_mask[:, b:b + 1], None, ALU.mult))
                    split(wred[:, b, 0, 16:32], wred[:, b, 1, 16:32], t_mw)
                def par(i):
                    return t_par[:, i:i + 1]
                link(dve.tensor_tensor(col(46), par(P_GAMMA), col(39), ALU.mult))
                link(dve.tensor_tensor(col(47), par(P_G), col(38), ALU.mult))
                link(dve.tensor_tensor(col(47), col(47), col(46), ALU.mult))
                link(dve.tensor_scalar(red_scale[:], col(47), col(42), 1.0 / (XS * WS), ALU.mult, ALU.mult))
                link(dve.tensor_tensor(col(48), par(P_B), par(P_MEAN), ALU.subtract))
                link(dve.tensor_tensor(col(48), col(48), col(46), ALU.mult))
                link(dve.tensor_tensor(red_bias[:], col(48), par(P_BETA), ALU.add))
                dve.tensor_copy(col(49), col(48)).then_inc(taps_ready, 1)
                for pos in range(POS):
                    dy, dx = pos // PX, pos % PX
                    dve.wait_ge(sel_ready, pos + 1)
                    dve.tensor_copy(
                        Wv[0:PATCH, :, :, dy, O * dx:O * (dx + 1)].rearrange("k l g o -> k (l g) o"),
                        Ybank[(pos % 4) // 2][0:PATCH, pos % 2, :].rearrange("k (n o) -> k n o", o=O)).then_inc(sel_read, 1)
                dve.wait_ge(sel_ready, POS + 1)
                dve.tensor_copy(wbias[0:PATCH, 0:64 * GROUPS].rearrange("k (n p) -> k n p", p=32)[:, :, 16:32],
                                Obank[0][0:PATCH, :].rearrange("k (p n) -> k n p", n=32)).then_inc(sel_read, 1)
            front_links = CHUNKS + 13
            counted_before = []

            def links_at(p):
                return 0 if isinstance(p, int) and p == 0 else counted_before[0] + front_links * (p - 1)

            def totals(p):
                dve.wait_ge(x_loaded, XLOAD * (p + 1))
                dve.tensor_reduce(col(S_SUM), slot(p), AX.X, ALU.add).then_inc(sum_ready, 1)

            def negative_mean(p):
                dve.wait_ge(m_ready, front_use(p, 0) + 1)
                dve.tensor_scalar(col(S_NMEAN), Mbank[0][:, 0:1], -1.0 / HW, None, ALU.mult).then_inc(m_read, 1)
                dve.wait_ge(m_read, front_use(p, 0) + 1)
                dve.tensor_copy(col(12), col(S_NMEAN)).then_inc(nmean_ready, 1)

            def chunk(p, k):
                if k == 0 and counted_before:
                    links[0] = 0
                base = links_at(p)
                rows = xs[:, bass.ds((p % 2) * HW + CW * k, CW)]
                dve.wait_ge(m_ready, front_use(p, 1 + k) + 1)
                dve.scalar_tensor_tensor(rows, Mbank[(1 + k) % 2][:, 0:CW], scale[:], rows, ALU.mult,
                                         ALU.add).then_inc(m_read, 1)
                written = known(dve, front_use(p, 1 + k) + 1)
                dve.wait_ge(first_loaded, FIRST_LOADS)
                dve.wait_ge(m_read, written)
                dve.bn_stats(bn[:, k, :], rows).then_inc(chain, 1)
                links[0] += 1
                counted = known(dve, base + links[0])
                dve.wait_ge(first_loaded, FIRST_LOADS)
                dve.wait_ge(chain, counted)
                if k == CHUNKS - 1:
                    dve.bn_aggr(mv[:], bn[:].rearrange("p a b -> p (a b)")).then_inc(stats_ready, 1)

            def spread(p):
                base = links_at(p)
                dve.wait_ge(m_ready, front_use(p, CHUNKS + 1) + 1)
                link(dve.tensor_copy(col(S_GM), Mbank[(CHUNKS + 1) % 2][:, 0:1]), base)
                link(dve.tensor_tensor(col(S_D), mv[:, 0:1], col(S_GM), ALU.subtract), base)
                link(dve.tensor_tensor(col(S_U), col(S_D), col(S_D), ALU.mult), base)
                dve.tensor_tensor(col(S_T), col(S_U), mv[:, 1:2], ALU.add).then_inc(stats_ready, 1)
                dve.wait_ge(stats_ready, 2 * (p + 1))
                link(dve.tensor_copy(col(13), col(S_T)), base)
                dve.tensor_copy(col(14), col(13)).then_inc(m_read, 1)

            def variance(p):
                base = links_at(p)
                dve.wait_ge(m_ready, front_use(p, CHUNKS + 2) + 1)
                link(dve.tensor_scalar(col(S_VE), Mbank[(CHUNKS + 2) % 2][:, 0:1], EPS, None, ALU.add), base)
                dve.tensor_copy(col(15), col(S_VE)).then_inc(var_ready, 1)

            def affine(p):
                base = links_at(p)
                dve.wait_ge(std_ready, p + 1)
                inv_root(col(S_Y), col(S_VE), col(S_SD), col(S_U), lambda ins: link(ins, base))
                link(dve.tensor_scalar(col(S_RS), col(S_Y), XS, None, ALU.mult), base)
                link(dve.tensor_tensor(col(16), col(S_GM), col(S_RS), ALU.mult), base)
                link(dve.tensor_scalar(col(S_NB), col(16), -1.0, None, ALU.mult), base)
                dve.tensor_copy(col(17), col(S_NB)).then_inc(affine_ready, 1)
                dve.tensor_copy(col(18), col(S_NB)).then_inc(m_read, 1)
                assert not counted_before or links[0] == front_links, links[0]

            def patches(p, behind):
                for n in range(T_ALL):
                    if behind:
                        for k in [k for k, after in BACK_AFTER.items() if after == n]:
                            added(p - 1, k, False)
                    if T_ON_DVE[n]:
                        part, q, s = tplace(n)
                        dve.wait_ge(t_ready, T_ALL * p + n + 1)
                        dve.tensor_copy(patch_rows(part, q, s).bitcast(U32),
                                        tbank(n)[0:PATCH, :].bitcast(U32)).then_inc(t_dve, 1)

            def product(p, g, q):
                u = Q * g + q
                dve.wait_ge(y_ready, 64 * p + u + 1)
                if u == 0:
                    dve.wait_ge(r_done, 4 * (p + 1))
                if q < 2:
                    dve.wait_ge(osum_done, GROUPS * p + g + 1 + q)
                dve.tensor_tensor(
                    prod[:, place(g, q), :].rearrange("m (d n c) -> m d n c", d=PY, c=GC),
                    Ybank[u % 2][:, :, 0:UNIT].rearrange("m d (n c) -> m d n c", c=GC),
                    R[:, :, q, :, :].rearrange("m d b j -> m d (b j)").unsqueeze(3).broadcast_to((128, PY, 2 * J, GC)),
                    ALU.mult).then_inc(prod_done, 1)

            def added(p, n, last):
                jys, strips = bplace(n)
                dve.wait_ge(m_ready, back_use(p, n, last) + 1)
                for h, jy in enumerate(jys):
                    for gp in range(2):
                        rows = xs[64 * gp:64 * gp + 64, bass.ds((p % 2) * HW + CW * jy, CW)].rearrange(
                            "p (y s x) -> p s y x", y=8, s=STRIPS)[:, strips[0]:strips[-1] + 1]
                        add = dve.tensor_tensor(
                            rows, bbank(n)[64 * h:64 * h + 64, 0:128 * len(strips)].rearrange(
                                "p (s g y x) -> p s g y x", g=2, y=8, x=8)[:, :, gp], rows, ALU.add)
                add.then_inc(m_read, 1)
                if n == BACK_M - 1:
                    dve.wait_ge(m_read, back_use(p, n, last) + 1)
                    dve.tensor_copy(col(19), col(S_NB)).then_inc(out_added, 1)

            totals(0)
            negative_mean(0)
            squares()
            for k in range(CHUNKS):
                chunk(0, k)
            spread(0)
            variance(0)
            affine(0)
            setup()
            counted_before.append(links[0])

            def step(p, more, behind):
                patches(p, behind)
                for g in range(GROUPS):
                    for q in range(Q):
                        product(p, g, q)
                        if more:
                            if (g, q) == (0, 3):
                                totals(p + 1)
                            if (g, q) == (1, 2):
                                negative_mean(p + 1)
                            if q == 3 and g in CONV_AT:
                                chunk(p + 1, CONV_AT[g])
                            if (g, q) == (10, 1):
                                spread(p + 1)
                            if (g, q) == (11, 2):
                                variance(p + 1)
                            if (g, q) == (12, 0):
                                affine(p + 1)

            step(0, True, False)
            if pairs > 2:
                with dve.Fori(1, pairs - 1) as p:
                    step(p, True, True)
            step(pairs - 1, False, True)
            for n in range(BACK_M):
                added(pairs - 1, n, True)


def constants():
    import numpy as np

    c = np.zeros((128, C_N), np.float32)
    c[:, C_ID:C_ID + 128] = np.eye(128)
    for dy in range(PY):
        for dx in range(PX):
            for ky in range(K):
                for kx in range(K):
                    c[ky * K + kx, C_SEL + (dy * PX + dx) * PATCH + (dy + ky) * IX + dx + kx] = 1
    for m in range(128):
        c[m, C_G + m // 2 * 2:C_G + m // 2 * 2 + 2] = 0.5
        c[m, C_E + 24 + m // O] = 1
        c[m, C_M + m // 32 % 2] = 1
    for q in range(Q):
        for gp in range(2):
            for dy in range(PY):
                for dx in range(PX):
                    c[32 * q + 16 * gp + PX * dy + dx, C_R + 64 * gp + 8 * (PY * q + dy) + dx] = 1
    return c


def layouts(w, scale, v_reduce, per_o, v_span, g_span, b_span):
    import numpy as np

    order = np.arange(C).reshape(C // 8, 2, GC).transpose(1, 0, 2).reshape(2, 32)
    at = np.repeat(order, 2, axis=0).reshape(128)
    p = np.zeros((128, P_N), np.float32)
    p[:, P_SCALE] = scale[at]
    for i, v in enumerate(per_o):
        p[:, P_G + i] = np.tile(v, PX)
    p[:, P_VT:P_VT + O] = v_reduce.T[at]
    p[:, P_ROW:P_ROW + C] = np.tile(v_reduce, (PX, 1))
    p[:, P_CONV:P_N] = w.transpose(1, 2, 3, 0)[at][..., order.reshape(C)].reshape(128, 9 * C)
    span = np.concatenate([v_span.reshape(TAPS, GROUPS * O), g_span.reshape(TAPS, GROUPS),
                           b_span.reshape(TAPS, GROUPS)], axis=1)
    gb = np.concatenate([g_span, b_span]).reshape(1, -1)
    return p, np.ascontiguousarray(span), gb, np.ascontiguousarray(v_reduce.reshape(1, -1))


def inputs_of(x, L0_conv_weight, L0_conv_scale, L1_conv_v_reduce, L1_conv_g_reduce, L1_conv_b_reduce,
              L1_conv_bn_gamma, L1_conv_bn_beta, L1_conv_bn_mean, L1_conv_bn_var, L1_conv_v_span,
              L1_conv_g_span, L1_conv_b_span):
    import numpy as np

    per_o = [np.asarray(a) for a in (L1_conv_g_reduce, L1_conv_b_reduce, L1_conv_bn_gamma, L1_conv_bn_beta,
                                     L1_conv_bn_mean, L1_conv_bn_var)]
    p, span, gb, vr = layouts(np.asarray(L0_conv_weight), np.asarray(L0_conv_scale), np.asarray(L1_conv_v_reduce),
                              per_o, np.asarray(L1_conv_v_span), np.asarray(L1_conv_g_span),
                              np.asarray(L1_conv_b_span))
    return {"x_dram": np.ascontiguousarray(x), "consts_dram": constants(), "params_dram": p, "span_dram": span,
            "gb_dram": gb, "vr_dram": vr}


def kernel(**inputs):
    import concourse.bacc as bacc
    from concourse.bass_utils import run_bass_kernel_spmd

    arrays = inputs_of(**inputs)
    nc = bacc.Bacc("TRN2", target_bir_lowering=False, num_devices=1)
    ins = [nc.dram_tensor(n, a.shape, mybir.dt.from_np(a.dtype), kind="ExternalInput").ap() for n, a in arrays.items()]
    out = nc.dram_tensor("out_dram", (B, C, H, W), F32, kind="ExternalOutput").ap()
    build(nc, *ins, out)
    r = run_bass_kernel_spmd(nc, [arrays], core_ids=[0])
    return r.results[0]["out_dram"]
```

```python
from contextlib import ExitStack

import concourse.bass as bass
from concourse import mybir

F32 = mybir.dt.float32
F16 = mybir.dt.float16
BF16 = mybir.dt.bfloat16
U32 = mybir.dt.uint32
ALU = mybir.AluOpType
ACT = mybir.ActivationFunctionType
AX = mybir.AxisListType

B, C, H, W = 32, 64, 56, 56
PAIRS = B // 2
HW = H * W
GROUPS, GC = 16, 4
O = 16
HALVES, OH = 2, 8
K, PAD = 7, 3
TAPS = K * K
PY, PX = 2, 8
POS = PY * PX
IY, IX = PY + K - 1, PX + K - 1
PATCH = IY * IX
STRIPS = W // PX
ROWS = H + 2 * PAD
STRIP = ROWS * IX
Q = 4
JY = H // (PY * Q)
J = JY * STRIPS
UNIT = 2 * J * GC
CR = 8
CHUNKS = H // CR
CW = CR * W
XS, WS = 256.0, 1024.0
EPS = 1e-5
TINY = 1e-30

C_ID, C_SEL = 0, 128
C_G = C_SEL + POS * PATCH
C_E = C_G + 128
C_R = C_E + 48
C_M = C_R + 128
C_N = C_M + 2
P_SCALE, P_G, P_B, P_GAMMA, P_BETA, P_MEAN, P_VAR, P_VT = range(8)
P_ROW = P_VT + O
P_CONV = P_ROW + C
P_N = P_CONV + 9 * C

FIRST_LOADS, LOADS, ZEROS = 16 * 2, 16 * 8, 4
XLOAD = 16 * 4
SPREAD = 16 * 4 * HALVES
FRONT_M, BACK_M = CHUNKS + 3, 8
T_ALL = 2 * Q * STRIPS
BACK_AFTER = {0: 2, 1: 5, 2: 8, 3: 11, 4: 14, 5: 17, 6: 20, 7: 23}
T_ON_DVE = [n % 5 in (1, 4) if n < 26 else n % 9 not in (0, 2, 4, 6) for n in range(T_ALL)]
SUM_AT = {(1, 2): 0, (2, 0): 1, (2, 2): 2, (3, 0): 3}
CONV_AT = {(4 + k // 2, 1 + 2 * (k % 2)): k for k in range(CHUNKS)}
MEAN_AT, VARIANCE_AT, AFFINE_AT = 8, 9, 10
LOW_AT = {(11, 2): 0, (12, 2): 2, (13, 2): 4, (14, 0): 5, (14, 2): 6}
POOL_LOW_AT = {(12, 1): 1, (13, 0): 3}
POOL_LOWS = sorted(POOL_LOW_AT.values())
N_POOL_LOWS, N_DVE_LOWS = len(POOL_LOWS), STRIPS - len(POOL_LOWS)


def build(nc, x, consts, params, span, gb_all, vr_all, out, pairs=PAIRS):
    xv = x.rearrange("(p b) (gh gp c) h w -> p gp b gh c (h w)", b=2, gp=2, c=GC)
    ov = out.rearrange("(p b) (gh gp c) h w -> p gp b gh c (h w)", b=2, gp=2, c=GC)

    with ExitStack() as ctx:
        def sb(name, shape, dt=F32):
            return ctx.enter_context(nc.sbuf_tensor(name, shape, dt))

        def sem(name):
            return ctx.enter_context(nc.semaphore(name))

        X = sb("patches", [128, 2 * Q * J * 128], F16)
        wspan = sb("wspan", [128, 2 * GROUPS * HALVES * 128], F16)
        wbias = sb("wbias", [128, 2 * GROUPS * 32 + 16], F16)
        S = sb("strips", [128, 2, STRIPS * STRIP], F16)
        xs = sb("xs", [128, 2 * HW])
        xn = sb("xn", [128, 2, H * IX])
        R = sb("relu", [128, HALVES, Q, 2, J])
        prod = sb("prod", [128, 2, HALVES, UNIT])
        rsum = prod[:].rearrange("p s h n -> p (s h n)").rearrange("p (i n) -> p i n", i=4)
        folded = sb("folded", [128, Q + 2, UNIT])
        osb = sb("osb", [128, J, C])
        ident = sb("ident", [128, 128], F16)
        gmat = sb("gmat", [128, 128])
        esum = sb("esum", [128, 48])
        back = sb("back", [128, 128])
        convw = sb("convw", [128, 9, 128], BF16)
        wred = sb("wred", [128, 2, 2, 32], F16)
        scale = sb("scale", [128, 1])
        red_scale = sb("red_scale", [128, 1])
        red_bias = sb("red_bias", [128, 1])
        alpha = sb("alpha", [128, 1])
        sm = sb("small", [128, 64])
        rowsums = sb("rowsums", [128, H])
        bn = sb("bn", [128, CHUNKS, 6])
        mv = sb("mv", [128, 2])
        sgn = S[:, 1, 0:(H + 2) * (W + 2)].bitcast(BF16)
        sgn3 = sgn.rearrange("p (h w) -> p h w", w=W + 2)

        Ybank = [ctx.enter_context(nc.psum_tensor(f"ybank{i}", [128, HALVES, 512], F32)) for i in range(3)]
        Obank = ctx.enter_context(nc.psum_tensor("obank", [128, 512], F32))
        Mbank = ctx.enter_context(nc.psum_tensor("mbank", [128, 512], F32))

        Xv = X[:].rearrange("k (l q j p) -> k l q j p", l=2, q=Q, p=128)
        Wv = wspan[:].rearrange("k (l g h m) -> k l g h m", l=2, g=GROUPS, h=HALVES)

        first_loaded = sem("first_loaded")
        setup_loaded = sem("setup_loaded")
        zeroed = sem("zeroed")
        setup_sqrt_in = sem("setup_sqrt_in")
        setup_sqrt_out = sem("setup_sqrt_out")
        convw_ready = sem("convw_ready")
        taps_ready = sem("taps_ready")
        sel_ready = sem("sel_ready")
        sel_read = sem("sel_read")
        chain = sem("chain")
        x_loaded = sem("x_loaded")
        stored = sem("stored")
        part_ready = sem("part_ready")
        sum_ready = sem("sum_ready")
        m_ready = sem("m_ready")
        m_read = sem("m_read")
        nmean_ready = sem("nmean_ready")
        sgn_zeroed = sem("sgn_zeroed")
        sgn_ready = sem("sgn_ready")
        stats_ready = sem("stats_ready")
        var_ready = sem("var_ready")
        std_ready = sem("std_ready")
        affine_ready = sem("affine_ready")
        low_zeroed = sem("low_zeroed")
        high_strip = sem("high_strip")
        low_dve = sem("low_dve")
        low_pool = sem("low_pool")
        r_ready = sem("r_ready")
        r_done = sem("r_done")
        r_spread = sem("r_spread")
        t_ready = sem("t_ready")
        t_act = sem("t_act")
        t_dve = sem("t_dve")
        y_ready = sem("y_ready")
        prod_done = sem("prod_done")
        fold_done = sem("fold_done")
        osum_done = sem("osum_done")
        o_ready = sem("o_ready")
        o_done = sem("o_done")
        out_added = sem("out_added")

        def slot(p, places=slice(0, 128)):
            return xs[places, bass.ds((p % 2) * HW, HW)]

        def front_use(p, k):
            if isinstance(p, int):
                return k if p == 0 else FRONT_M + (FRONT_M + BACK_M) * (p - 1) + k
            return (p - 1) * (FRONT_M + BACK_M) + FRONT_M + k

        def back_use(p, k, last):
            return p * (FRONT_M + BACK_M) + (FRONT_M if last else 2 * FRONT_M) + k

        def known(eng, value):
            return value if isinstance(value, int) else eng.to_reg(value)

        def place(g, q):
            return Q + q if q < 2 and g % 2 else q

        def tbank(n):
            return Ybank[(2, 1, 0)[n // 2 % 3]][:, n % 2, 0:STRIPS * 64].bitcast(F16)

        def ybank(u):
            return Ybank[{62: 0, 63: 2}.get(u, u % 3)]

        def before(u):
            return max(v for v in range(u) if ybank(v) is ybank(u))

        def fbank(p, k):
            return Obank if isinstance(p, int) and p == 0 and k % 2 else Mbank

        def tplace(n):
            return n // STRIPS % 2, n // (2 * STRIPS), n % STRIPS

        def strip_range(s):
            return (PAD if s == 0 else 0), (IX - PAD if s == STRIPS - 1 else IX)

        def strip(part, s):
            return S[:, part, s * STRIP + PAD * IX:s * STRIP + (PAD + H) * IX].rearrange("p (h w) -> p h w", w=IX)

        def inner(part):
            return S[:, part, :].rearrange("p (s h w) -> p s h w", h=ROWS, w=IX)[:, :, PAD:PAD + H]

        def rstrips(half):
            return range(4) if half == 0 else range(4, STRIPS)

        def xn3(s):
            return xn[:, s % 2, :].rearrange("p (h w) -> p h w", w=IX)

        def patch_rows(part, q, s):
            return Xv[0:PATCH, part, q, JY * s:JY * (s + 1), :].rearrange("k j p -> k (j p)")

        def bplace(n):
            return (range(2 * (n // 2), min(2 * (n // 2) + 2, JY)), range(4) if n % 2 == 0 else range(4, STRIPS))

        def bbank(n):
            return (Mbank, Obank)[n % 2]

        DVE_BEFORE = [sum(T_ON_DVE[:n]) for n in range(T_ALL + 1)]
        N_DVE, N_ACT = DVE_BEFORE[T_ALL], T_ALL - DVE_BEFORE[T_ALL]

        tmp = X[:].bitcast(F32)
        t_id, t_sel = tmp[:, 0:128], tmp[0:TAPS, 128:128 + POS * PATCH]
        t_span = tmp[0:TAPS, 2048:2048 + GROUPS * (O + 2)]
        t_gb = tmp[:, 2560:2560 + 2 * TAPS * GROUPS]
        t_vr = tmp[:, 4224:4224 + O * C]
        t_par = tmp[:, 5376:5376 + P_N]
        t_sq = tmp[0:TAPS, 6272:6528]
        t_ss = tmp[0:TAPS, 6528:6544]
        t_rt = tmp[0:TAPS, 6560:6576]
        t_rs = tmp[0:TAPS, 6592:6608]
        t_u = tmp[0:TAPS, 6624:6640]
        t_w = tmp[0:TAPS, 6656:6912]
        t_b = tmp[0:TAPS, 6912:6928]
        t_mask = tmp[:, 5354:5356]
        t_row = tmp[:, 6944:6944 + C]
        t_vw = tmp[:, 7088:7104]
        t_mw = tmp[:, 7104:7120]
        t_sel16 = X[0:TAPS, 16384:16384 + POS * PATCH]
        t_w16 = X[0:TAPS, 18432:18432 + 512].rearrange("t (l n) -> t l n", l=2)
        t_b16 = X[0:TAPS, 19200:19232].rearrange("t (l n) -> t l n", l=2)

        def col(i):
            return sm[:, i:i + 1]
        (S_SUM, S_NMEAN, S_GM, S_D, S_T, S_VE, S_SD, S_Y, S_U, S_RS, S_NB) = range(11)

        def cols(i, n):
            return sm[:, i:i + n]
        s_squares, s_roots, s_inverse, s_scratch = cols(20, 2), cols(22, 2), cols(24, 2), cols(26, 2)

        block = ctx.enter_context(nc.Block())

        @block.sync
        def _(sp):
            def load(p, into):
                for gp in range(2):
                    for b in range(2):
                        sp.dma_start(into[64 * gp + 32 * b:64 * gp + 32 * b + 32], xv[p][gp][b]).then_inc(x_loaded, 16)

            sp.dma_start(gmat[:], consts[:, C_G:C_E]).then_inc(first_loaded, 16)
            sp.dma_start(t_par, params).then_inc(first_loaded, 16)
            load(0, xs[:, 0:HW])
            for dst, src in ((t_id, consts[:, C_ID:C_ID + 128]), (t_sel, consts[0:TAPS, C_SEL:C_G]),
                             (esum[:], consts[:, C_E:C_R]), (back[:], consts[:, C_R:C_M]), (t_mask, consts[:, C_M:C_N]),
                             (t_span, span), (t_gb, gb_all.broadcast_to((128, 2 * TAPS * GROUPS))),
                             (t_vr, vr_all.broadcast_to((128, O * C)))):
                sp.dma_start(dst, src).then_inc(setup_loaded, 16)
            sp.wait_ge(x_loaded, XLOAD)
            load(1, xs[:, HW:2 * HW])

            def spread(p):
                sp.wait_ge(r_done, 4 * (p + 1))
                for t in range(4):
                    for h in range(HALVES):
                        row = 32 * t + OH * h
                        sp.dma_start(R[32 * t:32 * t + 32, h].rearrange("m q b j -> m (q b j)"),
                                     rsum[row:row + OH]).then_inc(r_spread, 16)

            spread(0)

            def step(p, load_next, more):
                if more:
                    spread(p + 1)
                sp.wait_ge(out_added, p + 1)
                for gp in range(2):
                    for b in range(2):
                        quarter = slice(64 * gp + 32 * b, 64 * gp + 32 * b + 32)
                        sp.dma_start(ov[p][gp][b], slot(p, quarter)).then_inc(stored, 16)
                there, loaded = known(sp, XLOAD * (p + 1)), known(sp, XLOAD * (p + 2))
                sp.wait_ge(x_loaded, XLOAD)
                sp.wait_ge(stored, there)
                if load_next:
                    sp.wait_ge(x_loaded, loaded)
                    for gp in range(2):
                        for b in range(2):
                            quarter = slice(64 * gp + 32 * b, 64 * gp + 32 * b + 32)
                            sp.dma_start(slot(p, quarter), xv[p + 2][gp][b]).then_inc(x_loaded, 16)

            if pairs > 2:
                with sp.Fori(0, pairs - 2) as p:
                    step(p, True, True)
            step(pairs - 2, False, True)
            step(pairs - 1, False, False)

        @block.gpsimd
        def _(pool):
            pool.memset(S[:].rearrange("p l n -> p (l n)").bitcast(U32), 0).then_inc(zeroed, 1)
            pool.memset(wbias[:].bitcast(U32), 0).then_inc(zeroed, 1)
            pool.memset(wred[:].rearrange("p a b c -> p (a b c)").bitcast(U32), 0).then_inc(zeroed, 1)
            pool.memset(convw[:].rearrange("p a b -> p (a b)").bitcast(U32), 0).then_inc(zeroed, 1)
            pool.wait_ge(zeroed, ZEROS)

            def signs_border(p):
                transposed = known(pool, T_ALL * p)
                pool.wait_ge(zeroed, ZEROS)
                if not (isinstance(p, int) and p == 0):
                    pool.wait_ge(t_ready, transposed)
                pool.memset(sgn.bitcast(U32), 0).then_inc(sgn_zeroed, 1)

            def low_border(p):
                convolved = known(pool, front_use(p, CHUNKS) + 1)
                pool.wait_ge(zeroed, ZEROS)
                pool.wait_ge(m_ready, convolved)
                pool.memset(S[:, 1, :].bitcast(U32), 0).then_inc(low_zeroed, 1)

            def low(p, s, done):
                lo, hi = strip_range(s)
                pool.wait_ge(low_zeroed, p + 1)
                pool.wait_ge(high_strip, STRIPS * p + s + 1)
                pool.tensor_tensor(strip(1, s)[:, :, lo:hi], xn3(s)[:, :, lo:hi], strip(0, s)[:, :, lo:hi],
                                   ALU.subtract).then_inc(done, 1)

            def first_low():
                for s in range(STRIPS):
                    low(0, s, low_pool if s in POOL_LOWS else low_dve)

            def fold(p, g, q):
                u = Q * g + q
                pool.wait_ge(prod_done, 64 * p + u + 1)
                if q in (0, 2):
                    pool.wait_ge(osum_done, GROUPS * p + g + 1 + q // 2)
                pool.tensor_tensor(folded[:, place(g, q), :], prod[:, u % 2, 0, :], prod[:, u % 2, 1, :],
                                   ALU.add).then_inc(fold_done, 1)

            def step(p, more):
                if more:
                    signs_border(p + 1)
                for g in range(GROUPS):
                    for q in range(Q):
                        fold(p, g, q)
                        if more:
                            if (g, q) == (MEAN_AT, 1):
                                low_border(p + 1)
                            if (g, q) in POOL_LOW_AT:
                                low(p + 1, POOL_LOW_AT[g, q], low_pool)

            signs_border(0)
            low_border(0)
            first_low()
            with pool.Fori(0, pairs - 1) as p:
                step(p, True)
            step(pairs - 1, False)

        @block.scalar
        def _(act):
            act.wait_ge(first_loaded, FIRST_LOADS)
            act.wait_ge(zeroed, ZEROS)
            for place_in in range(0, 128, 32):
                image = place_in // 32 % 2
                for gp in range(2):
                    act.activation(convw[place_in:place_in + 32, :, 64 * gp + 32 * image:64 * gp + 32 * image + 32],
                                   t_par[place_in:place_in + 32, P_CONV:P_N].rearrange(
                                       "p (t o) -> p t o", t=9)[:, :, 32 * gp:32 * gp + 32],
                                   ACT.Sign).then_inc(convw_ready, 1)

            def setup_roots():
                act.wait_ge(setup_sqrt_in, 1)
                act.activation(t_rt, t_ss, ACT.Sqrt).then_inc(setup_sqrt_out, 1)
                act.activation(s_roots, s_squares, ACT.Sqrt).then_inc(setup_sqrt_out, 1)
                act.wait_ge(setup_sqrt_out, 2)
                act.activation(col(60), col(22), ACT.Copy).then_inc(o_done, 1)

            def sign(p):
                turn = known(act, p + 1)
                act.wait_ge(first_loaded, FIRST_LOADS)
                act.wait_ge(nmean_ready, turn)
                act.wait_ge(sgn_zeroed, turn)
                act.activation(sgn3[:, 1:H + 1, 1:W + 1], slot(p).rearrange("p (h w) -> p h w", w=W),
                               ACT.Sign, bias=col(S_NMEAN)).then_inc(sgn_ready, 1)

            def root(p):
                act.wait_ge(var_ready, p + 1)
                act.activation(col(S_SD), col(S_VE), ACT.Sqrt).then_inc(std_ready, 1)

            def strips(p, some):
                act.wait_ge(affine_ready, p + 1)
                if not (isinstance(p, int) and p == 0):
                    act.wait_ge(t_ready, T_ALL * p)
                x3 = slot(p).rearrange("p (h w) -> p h w", w=W)
                for s in some:
                    lo, hi = strip_range(s)
                    src = x3[:, :, PX * s - PAD + lo:PX * s - PAD + hi]
                    last = s - 2 if s >= 2 else (STRIPS - 1, STRIPS - 2)[s]
                    on_pool = last in POOL_LOWS
                    count = sum((t in POOL_LOWS) == on_pool for t in range(s - 1))
                    read = known(act, (N_POOL_LOWS if on_pool else N_DVE_LOWS) * p + count)
                    act.wait_ge(zeroed, ZEROS)
                    if not (isinstance(read, int) and read == 0):
                        act.wait_ge(low_pool if on_pool else low_dve, read)
                    act.activation(xn3(s)[:, :, lo:hi], src, ACT.Identity, bias=col(S_NB), scale=col(S_RS))
                    act.activation(strip(0, s)[:, :, lo:hi], src, ACT.Identity, bias=col(S_NB),
                                   scale=col(S_RS)).then_inc(high_strip, 1)

            def relus(p):
                if not (isinstance(p, int) and p == 0):
                    act.wait_ge(fold_done, 64 * p)
                for k in range(4):
                    b, half = k // 2, k % 2
                    strips = rstrips(half)
                    act.wait_ge(r_ready, 4 * p + k + 1)
                    act.activation(
                        rsum.rearrange("m i (q b j) -> m b j q i", q=Q, b=2)[:, b, JY * strips[0]:JY * (strips[-1] + 1)],
                        Ybank[1 - b][:, half, 0:16 * JY * len(strips)].rearrange("m (j q i) -> m j q i", q=Q, i=4),
                        ACT.Relu, bias=red_bias[:], scale=red_scale[:]).then_inc(r_done, 1)

            def patches(p):
                for n in range(T_ALL):
                    if not T_ON_DVE[n]:
                        part, q, s = tplace(n)
                        act.wait_ge(t_ready, T_ALL * p + n + 1)
                        act.activation(patch_rows(part, q, s), tbank(n)[0:PATCH, :], ACT.Copy).then_inc(t_act, 1)

            def gather(p, G):
                if G == 0:
                    act.wait_ge(m_ready, FRONT_M + (FRONT_M + BACK_M) * p)
                act.wait_ge(o_ready, 8 * p + G + 1)
                act.activation(osb[:].rearrange("m j (b g c) -> m b j g c", b=2, c=GC)[:, :, :, G, :],
                               Obank[:, 0:UNIT].rearrange("m (b j c) -> m b j c", b=2, c=GC),
                               ACT.Copy, scale=alpha[:]).then_inc(o_done, 1)

            sign(0)
            setup_roots()
            root(0)
            strips(0, range(STRIPS))
            act.wait_ge(taps_ready, 1)
            relus(0)
            act.wait_ge(sel_read, POS + 1)

            def step(p, more):
                patches(p)
                gather(p, 0)
                if more:
                    sign(p + 1)
                for G in range(1, 4):
                    gather(p, G)
                if more:
                    root(p + 1)
                gather(p, 4)
                if more:
                    strips(p + 1, range(4))
                gather(p, 5)
                if more:
                    strips(p + 1, range(4, STRIPS))
                gather(p, 6)
                if more:
                    relus(p + 1)
                gather(p, 7)

            with act.Fori(0, pairs - 1) as p:
                step(p, True)
            step(pairs - 1, False)

        @block.tensor
        def _(pe):
            def select():
                pe.wait_ge(taps_ready, 1)
                for pos in range(POS):
                    if pos >= 4:
                        pe.wait_ge(sel_read, pos - 3)
                    pe.matmul(Ybank[(pos % 4) // 2][0:PATCH, pos % 2, :], t_sel16[:, PATCH * pos:PATCH * (pos + 1)],
                              t_w16.rearrange("t l n -> t (l n)"), start=True, stop=True).then_inc(sel_ready, 1)
                for pos in range(POS):
                    mm = pe.matmul(Obank[0:PATCH, 32 * pos:32 * pos + 32],
                                   t_sel16[:, PATCH * pos:PATCH * (pos + 1)],
                                   t_b16.rearrange("t l n -> t (l n)"), start=True, stop=True)
                    if pos < 2:
                        mm.then_inc(osum_done, 1)
                mm.then_inc(sel_ready, 1)

            def m_free(p, k):
                use = front_use(p, k)
                if isinstance(p, int) and p == 0:
                    if k >= 2:
                        pe.wait_ge(m_read, k - 1)
                else:
                    pe.wait_ge(m_read, use)

            def stat0(p):
                if isinstance(p, int) and p == 0:
                    pe.wait_ge(first_loaded, FIRST_LOADS)
                pe.wait_ge(sum_ready, p + 1)
                m_free(p, 0)
                pe.matmul(fbank(p, 0)[:, 0:1], gmat[:], col(S_SUM), start=True, stop=True).then_inc(m_ready, 1)

            def conv(p, k):
                if k == 0:
                    pe.wait_ge(convw_ready, 8)
                    pe.wait_ge(sgn_ready, p + 1)
                m_free(p, 1 + k)
                for tap in range(9):
                    dh, dw = tap // 3, tap % 3
                    mm = pe.matmul(fbank(p, 1 + k)[:, 0:CW], convw[:, tap, :],
                                   sgn3[:, CR * k + dh:CR * k + dh + CR, dw:dw + W], start=(tap == 0), stop=(tap == 8))
                mm.then_inc(m_ready, 1)

            def stat(p, n):
                pe.wait_ge(stats_ready, 2 * p + n)
                m_free(p, CHUNKS + n)
                pe.matmul(fbank(p, CHUNKS + n)[:, 0:1], gmat[:], mv[:, 0:1] if n == 1 else col(S_T),
                          start=True, stop=True).then_inc(m_ready, 1)

            def reduce(p):
                pe.wait_ge(high_strip, STRIPS * (p + 1))
                pe.wait_ge(low_dve, N_DVE_LOWS * (p + 1))
                pe.wait_ge(low_pool, N_POOL_LOWS * (p + 1))
                for b in range(2):
                    if not (isinstance(p, int) and p == 0):
                        pe.wait_ge(prod_done, 64 * p - 2 + b)
                    for half in range(2):
                        strips = rstrips(half)
                        for n, (wpart, xpart) in enumerate(((0, 0), (1, 0), (0, 1))):
                            for t in range(4):
                                dy, dx = t // 2, 4 * (t % 2)
                                rhs = inner(xpart)[:, strips[0]:strips[-1] + 1, dy:H:PY, PAD + dx:PAD + dx + 4]
                                mm = pe.matmul(Ybank[1 - b][32 * t:32 * t + 32, half, 0:16 * JY * len(strips)],
                                               wred[:, b, wpart, :], rhs, start=(n == 0), stop=(n == 2))
                        mm.then_inc(r_ready, 1)

            def transposes(p, behind):
                for n in range(T_ALL):
                    if behind:
                        for k in [k for k, after in BACK_AFTER.items() if after == n]:
                            block(p - 1, k, False)
                    if n == 0 and not (isinstance(p, int) and p == 0):
                        pe.wait_ge(prod_done, 64 * p)
                    if 2 <= n < 6:
                        pe.wait_ge(r_done, 4 * p + n - 1)
                    part, q, s = tplace(n)
                    if n >= 6:
                        copied = n - 5
                        if T_ON_DVE[copied - 1]:
                            pe.wait_ge(t_dve, N_DVE * p + DVE_BEFORE[copied])
                        else:
                            pe.wait_ge(t_act, N_ACT * p + copied - DVE_BEFORE[copied])
                    for jy in range(JY):
                        first = s * STRIP + PY * (Q * jy + q) * IX
                        mm = pe.transpose(tbank(n)[0:PATCH, 128 * jy:128 * (jy + 1)],
                                          S[:, part, first:first + PATCH], ident[:])
                    mm.then_inc(t_ready, 1)

            def of_group(xpart, q, g):
                return Xv[0:PATCH, xpart, q, :, :].rearrange("k j (gp b g c) -> k gp g b j c", gp=2, b=2, c=GC)[
                    :, g % 2, g // 2]

            def taps(p, g, q):
                u = Q * g + q
                if u >= 3:
                    pe.wait_ge(prod_done, 64 * p + before(u) + 1)
                else:
                    done = T_ALL - 2 + 2 * (u == 2)
                    pe.wait_ge(t_dve, N_DVE * p + DVE_BEFORE[done])
                    pe.wait_ge(t_act, N_ACT * p + done - DVE_BEFORE[done])
                for h in range(HALVES):
                    for n, (wpart, xpart) in enumerate(((0, 0), (1, 0), (0, 1))):
                        mm = pe.matmul(ybank(u)[:, h, 0:UNIT], Wv[0:PATCH, wpart, g, h, :], of_group(xpart, q, g),
                                       start=(n == 0), stop=(n == 2))
                mm.then_inc(y_ready, 1)

            def sums(p, g):
                G, gp = g // 2, g % 2
                pe.wait_ge(fold_done, 64 * p + Q * (g + 1))
                if g % 2 == 0:
                    pe.wait_ge(o_done, 8 * p + G + 1)
                    if G == 0:
                        pe.wait_ge(m_read, FRONT_M + (FRONT_M + BACK_M) * p)
                for q in range(Q):
                    mm = pe.matmul(Obank[32 * q:32 * q + 32, 0:UNIT], esum[:, 16 - 16 * gp:48 - 16 * gp],
                                   folded[:, place(g, q), :], start=(gp == 0), stop=False)
                mm.then_inc(osum_done, 1)
                for n, (wpart, xpart) in enumerate(((0, 0), (1, 0), (0, 1))):
                    w0 = 32 * (GROUPS * wpart + g) + 16 - 16 * gp
                    for q in range(Q):
                        mm = pe.matmul(Obank[32 * q:32 * q + 32, 0:UNIT], wbias[0:PATCH, w0:w0 + 32],
                                       of_group(xpart, q, g), start=False, stop=(gp == 1 and n == 2))
                if g % 2 == 1:
                    mm.then_inc(o_ready, 1)

            def block(p, n, last):
                read = known(pe, back_use(p, max(n - 1, 0), last))
                gathered = known(pe, 8 * (p + 1) + 1)
                pe.wait_ge(sel_read, POS + 1)
                if n == 0:
                    pe.wait_ge(o_done, gathered)
                pe.wait_ge(m_read, read)
                jys, strips = bplace(n)
                for i, st in enumerate(strips):
                    mm = pe.transpose(bbank(n)[0:64 * len(jys), 128 * i:128 * (i + 1)],
                                      osb[:, JY * st + jys[0]:JY * st + jys[0] + len(jys), :].rearrange(
                                          "m j c -> m (j c)"), back[:])
                mm.then_inc(m_ready, 1)

            stat0(0)
            for k in range(CHUNKS):
                conv(0, k)
            stat(0, 1)
            stat(0, 2)
            select()
            pe.wait_ge(sel_read, POS + 1)
            reduce(0)

            def step(p, more, behind):
                transposes(p, behind)
                for g in range(GROUPS):
                    taps(p, g, 0)
                    taps(p, g, 1)
                    if more and (g, 1) in CONV_AT:
                        conv(p + 1, CONV_AT[g, 1])
                        if g >= 1:
                            sums(p, g - 1)
                        taps(p, g, 2)
                    else:
                        taps(p, g, 2)
                        if more:
                            if g == 3:
                                stat0(p + 1)
                            if g == MEAN_AT:
                                stat(p + 1, 1)
                            if g == VARIANCE_AT:
                                stat(p + 1, 2)
                        if g >= 1:
                            sums(p, g - 1)
                    if more and (g, 3) in CONV_AT:
                        conv(p + 1, CONV_AT[g, 3])
                    taps(p, g, 3)
                if more:
                    reduce(p + 1)
                sums(p, GROUPS - 1)

            step(0, True, False)
            if pairs > 2:
                with pe.Fori(1, pairs - 1) as p:
                    step(p, True, True)
            step(pairs - 1, False, True)
            for n in range(BACK_M):
                block(pairs - 1, n, True)

        @block.vector
        def _(dve):
            links = [0]

            def link(ins, base=0):
                links[0] += 1
                ins.then_inc(chain, 1)
                dve.wait_ge(chain, base + links[0])

            def inv_root(y, v, root, u, lk):
                lk(dve.reciprocal(y, root))
                lk(dve.tensor_tensor(u, y, y, ALU.mult))
                lk(dve.tensor_tensor(u, u, v, ALU.mult))
                lk(dve.tensor_scalar(u, u, -0.5, 1.5, ALU.mult, ALU.add))
                lk(dve.tensor_tensor(y, y, u, ALU.mult))

            def max_of(dst, src, width):
                link(dve.tensor_reduce(dst, src, AX.X, ALU.max, apply_absolute_value=True))
                link(dve.tensor_scalar(dst, dst, TINY, None, ALU.max))

            def split(high, low, src):
                link(dve.tensor_copy(high, src))
                link(dve.tensor_tensor(low, src, high, ALU.subtract))

            sv = t_span[:, 0:GROUPS * O]

            def squares():
                dve.wait_ge(first_loaded, FIRST_LOADS)
                dve.wait_ge(setup_loaded, LOADS)
                link(dve.tensor_copy(scale[:], t_par[:, P_SCALE:P_SCALE + 1]))
                link(dve.tensor_tensor(t_sq, sv, sv, ALU.mult))
                link(dve.tensor_reduce(t_ss, t_sq.rearrange("t (g o) -> t g o", o=O), AX.X, ALU.add))
                vrow = t_par[:, P_ROW:P_ROW + C]
                link(dve.tensor_tensor(t_row, vrow, vrow, ALU.mult))
                link(dve.tensor_reduce(s_squares[:, 0:1], t_row, AX.X, ALU.add))
                dve.tensor_scalar(s_squares[:, 1:2], t_par[:, P_VAR:P_VAR + 1], EPS, None,
                                  ALU.add).then_inc(setup_sqrt_in, 1)

            def largest():
                link(dve.tensor_copy(ident[:], t_id))
                link(dve.tensor_copy(t_sel16, t_sel))
                max_of(col(40), t_gb, 2 * TAPS * GROUPS)
                link(dve.reciprocal(col(41), col(40)))
                link(dve.tensor_scalar(alpha[:], col(40), 1.0 / (XS * WS), None, ALU.mult))
                max_of(col(42), t_vr, O * C)
                link(dve.reciprocal(col(43), col(42)))

            def setup():
                dve.wait_ge(zeroed, ZEROS)
                dve.wait_ge(setup_sqrt_out, 2)
                inv_root(t_rs, t_ss, t_rt, t_u, link)
                inv_root(s_inverse, s_squares, s_roots, s_scratch, link)
                gs, bs = t_span[:, GROUPS * O:GROUPS * (O + 1)], t_span[:, GROUPS * (O + 1):GROUPS * (O + 2)]
                link(dve.tensor_scalar(t_u, gs, sm[0:TAPS, 41:42], WS, ALU.mult, ALU.mult))
                link(dve.tensor_tensor(t_u, t_u, t_rs, ALU.mult))
                link(dve.tensor_tensor(t_w.rearrange("t (g o) -> t g o", o=O), sv.rearrange("t (g o) -> t g o", o=O),
                                       t_u.unsqueeze(2).broadcast_to((TAPS, GROUPS, O)), ALU.mult))
                link(dve.tensor_scalar(t_b, bs, sm[0:TAPS, 41:42], WS, ALU.mult, ALU.mult))
                split(t_w16[:, 0, :], t_w16[:, 1, :], t_w)
                split(t_b16[:, 0, :], t_b16[:, 1, :], t_b)
                link(dve.tensor_scalar(t_vw, t_par[:, P_VT:P_VT + O], col(43), WS, ALU.mult, ALU.mult))
                for b in range(2):
                    link(dve.tensor_scalar(t_mw, t_vw, t_mask[:, b:b + 1], None, ALU.mult))
                    split(wred[:, b, 0, 0:O], wred[:, b, 1, 0:O], t_mw)
                def par(i):
                    return t_par[:, i:i + 1]
                norm, deviation = s_inverse[:, 0:1], s_inverse[:, 1:2]
                u, v, w = col(50), col(51), col(52)
                link(dve.tensor_tensor(u, par(P_GAMMA), deviation, ALU.mult))
                link(dve.tensor_tensor(v, par(P_G), norm, ALU.mult))
                link(dve.tensor_tensor(v, v, u, ALU.mult))
                link(dve.tensor_scalar(red_scale[:], v, col(42), 1.0 / (XS * WS), ALU.mult, ALU.mult))
                link(dve.tensor_tensor(w, par(P_B), par(P_MEAN), ALU.subtract))
                link(dve.tensor_tensor(w, w, u, ALU.mult))
                link(dve.tensor_tensor(red_bias[:], w, par(P_BETA), ALU.add))
                dve.tensor_copy(col(53), w).then_inc(taps_ready, 1)
                for pos in range(POS):
                    dve.wait_ge(sel_ready, pos + 1)
                    dve.tensor_copy(
                        Wv[0:PATCH, :, :, :, 32 * (pos // 4) + pos % 4:32 * (pos // 4 + 1):4].rearrange("k l g h o -> k (l g h) o"),
                        Ybank[(pos % 4) // 2][0:PATCH, pos % 2, :].rearrange("k (n o) -> k n o", o=OH)).then_inc(sel_read, 1)
                dve.wait_ge(sel_ready, POS + 1)
                dve.tensor_copy(wbias[0:PATCH, 0:64 * GROUPS].rearrange("k (n p) -> k n p", p=32)[:, :, 16:32],
                                Obank[0:PATCH, :].rearrange("k (p n) -> k n p", n=32)).then_inc(sel_read, 1)
            front_links = CHUNKS + 13
            counted_before = []

            def links_at(p):
                return 0 if isinstance(p, int) and p == 0 else counted_before[0] + front_links * (p - 1)

            def totals(p, k):
                dve.wait_ge(x_loaded, XLOAD * (p + 1))
                dve.tensor_reduce(rowsums[:, H // 4 * k:H // 4 * (k + 1)],
                                  xs[:, bass.ds((p % 2) * HW + HW // 4 * k, HW // 4)].rearrange(
                                      "p (h w) -> p h w", w=W), AX.X, ALU.add).then_inc(part_ready, 1)
                if k == 3:
                    dve.wait_ge(part_ready, 4 * (p + 1))
                    dve.tensor_reduce(col(S_SUM), rowsums[:], AX.X, ALU.add).then_inc(sum_ready, 1)

            def negative_mean(p):
                dve.wait_ge(m_ready, front_use(p, 0) + 1)
                dve.tensor_scalar(col(S_NMEAN), fbank(p, 0)[:, 0:1], -1.0 / HW, None, ALU.mult).then_inc(m_read, 1)
                dve.wait_ge(m_read, front_use(p, 0) + 1)
                dve.tensor_copy(col(12), col(S_NMEAN)).then_inc(nmean_ready, 1)

            def chunk(p, k):
                if k == 0 and counted_before:
                    links[0] = 0
                base = links_at(p)
                rows = xs[:, bass.ds((p % 2) * HW + CW * k, CW)]
                dve.wait_ge(m_ready, front_use(p, 1 + k) + 1)
                dve.scalar_tensor_tensor(rows, fbank(p, 1 + k)[:, 0:CW], scale[:], rows, ALU.mult,
                                         ALU.add).then_inc(m_read, 1)
                written = known(dve, front_use(p, 1 + k) + 1)
                dve.wait_ge(first_loaded, FIRST_LOADS)
                dve.wait_ge(m_read, written)
                dve.bn_stats(bn[:, k, :], rows).then_inc(chain, 1)
                links[0] += 1
                counted = known(dve, base + links[0])
                dve.wait_ge(first_loaded, FIRST_LOADS)
                dve.wait_ge(chain, counted)
                if k == CHUNKS - 1:
                    dve.bn_aggr(mv[:], bn[:].rearrange("p a b -> p (a b)")).then_inc(stats_ready, 1)

            def spread(p):
                base = links_at(p)
                dve.wait_ge(m_ready, front_use(p, CHUNKS + 1) + 1)
                link(dve.tensor_copy(col(S_GM), fbank(p, CHUNKS + 1)[:, 0:1]), base)
                link(dve.tensor_tensor(col(S_D), mv[:, 0:1], col(S_GM), ALU.subtract), base)
                link(dve.tensor_tensor(col(S_U), col(S_D), col(S_D), ALU.mult), base)
                dve.tensor_tensor(col(S_T), col(S_U), mv[:, 1:2], ALU.add).then_inc(stats_ready, 1)
                dve.wait_ge(stats_ready, 2 * (p + 1))
                link(dve.tensor_copy(col(13), col(S_T)), base)
                dve.tensor_copy(col(14), col(13)).then_inc(m_read, 1)

            def variance(p):
                base = links_at(p)
                dve.wait_ge(m_ready, front_use(p, CHUNKS + 2) + 1)
                link(dve.tensor_scalar(col(S_VE), fbank(p, CHUNKS + 2)[:, 0:1], EPS, None, ALU.add), base)
                dve.tensor_copy(col(15), col(S_VE)).then_inc(var_ready, 1)

            def affine(p):
                base = links_at(p)
                dve.wait_ge(std_ready, p + 1)
                inv_root(col(S_Y), col(S_VE), col(S_SD), col(S_U), lambda ins: link(ins, base))
                link(dve.tensor_scalar(col(S_RS), col(S_Y), XS, None, ALU.mult), base)
                link(dve.tensor_tensor(col(16), col(S_GM), col(S_RS), ALU.mult), base)
                link(dve.tensor_scalar(col(S_NB), col(16), -1.0, None, ALU.mult), base)
                dve.tensor_copy(col(17), col(S_NB)).then_inc(affine_ready, 1)
                dve.tensor_copy(col(18), col(S_NB)).then_inc(m_read, 1)
                assert not counted_before or links[0] == front_links, links[0]

            def low(p, s):
                lo, hi = strip_range(s)
                dve.wait_ge(low_zeroed, p + 1)
                dve.wait_ge(high_strip, STRIPS * p + s + 1)
                dve.tensor_tensor(strip(1, s)[:, :, lo:hi], xn3(s)[:, :, lo:hi], strip(0, s)[:, :, lo:hi],
                                  ALU.subtract).then_inc(low_dve, 1)

            def patches(p, behind):
                for n in range(T_ALL):
                    if behind:
                        for k in [k for k, after in BACK_AFTER.items() if after == n]:
                            added(p - 1, k, False)
                    if T_ON_DVE[n]:
                        part, q, s = tplace(n)
                        dve.wait_ge(t_ready, T_ALL * p + n + 1)
                        dve.tensor_copy(patch_rows(part, q, s).bitcast(U32),
                                        tbank(n)[0:PATCH, :].bitcast(U32)).then_inc(t_dve, 1)

            def product(p, g, q):
                u = Q * g + q
                dve.wait_ge(y_ready, 64 * p + u + 1)
                if u == 0:
                    dve.wait_ge(r_spread, SPREAD * (p + 1))
                if not (isinstance(p, int) and p == 0 and u < 2):
                    dve.wait_ge(fold_done, 64 * p + u - 1)
                dve.tensor_tensor(
                    prod[:, u % 2].rearrange("m h (n c) -> m h n c", c=GC),
                    ybank(u)[:, :, 0:UNIT].rearrange("m h (n c) -> m h n c", c=GC),
                    R[:, :, q, :, :].rearrange("m h b j -> m h (b j)").unsqueeze(3).broadcast_to((128, HALVES, 2 * J, GC)),
                    ALU.mult).then_inc(prod_done, 1)

            def added(p, n, last):
                jys, strips = bplace(n)
                dve.wait_ge(m_ready, back_use(p, n, last) + 1)
                for h, jy in enumerate(jys):
                    for gp in range(2):
                        rows = xs[64 * gp:64 * gp + 64, bass.ds((p % 2) * HW + CW * jy, CW)].rearrange(
                            "p (y s x) -> p s y x", y=8, s=STRIPS)[:, strips[0]:strips[-1] + 1]
                        add = dve.tensor_tensor(
                            rows, bbank(n)[64 * h:64 * h + 64, 0:128 * len(strips)].rearrange(
                                "p (s g y x) -> p s g y x", g=2, y=8, x=8)[:, :, gp], rows, ALU.add)
                add.then_inc(m_read, 1)
                if n == BACK_M - 1:
                    dve.wait_ge(m_read, back_use(p, n, last) + 1)
                    dve.tensor_copy(col(19), col(S_NB)).then_inc(out_added, 1)

            for k in range(4):
                totals(0, k)
            negative_mean(0)
            squares()
            largest()
            for k in range(CHUNKS):
                chunk(0, k)
            spread(0)
            variance(0)
            affine(0)
            setup()
            counted_before.append(links[0])

            def step(p, more, behind):
                patches(p, behind)
                for g in range(GROUPS):
                    for q in range(Q):
                        product(p, g, q)
                        if more:
                            if (g, q) in SUM_AT:
                                totals(p + 1, SUM_AT[g, q])
                            if (g, q) == (3, 2):
                                negative_mean(p + 1)
                            if (g, q) in CONV_AT:
                                chunk(p + 1, CONV_AT[g, q])
                            if (g, q) == (MEAN_AT, 2):
                                spread(p + 1)
                            if (g, q) == (VARIANCE_AT, 2):
                                variance(p + 1)
                            if (g, q) == (AFFINE_AT, 2):
                                affine(p + 1)
                            if (g, q) in LOW_AT:
                                low(p + 1, LOW_AT[g, q])

            step(0, True, False)
            if pairs > 2:
                with dve.Fori(1, pairs - 1) as p:
                    step(p, True, True)
            step(pairs - 1, False, True)
            for n in range(BACK_M):
                added(pairs - 1, n, True)


def constants():
    import numpy as np

    c = np.zeros((128, C_N), np.float32)
    c[:, C_ID:C_ID + 128] = np.eye(128)
    for dy in range(PY):
        for dx in range(PX):
            for ky in range(K):
                for kx in range(K):
                    c[ky * K + kx, C_SEL + (dy * PX + dx) * PATCH + (dy + ky) * IX + dx + kx] = 1
    for m in range(128):
        c[m, C_G + m // 2 * 2:C_G + m // 2 * 2 + 2] = 0.5
        c[m, C_E + 16 + 4 * (m // 32) + m % 4] = 1
        c[m, C_M + m // 32 % 2] = 1
    for q in range(Q):
        for gp in range(2):
            for dy in range(PY):
                for dx in range(PX):
                    c[32 * q + 16 * gp + PX * dy + dx, C_R + 64 * gp + 8 * (PY * q + dy) + dx] = 1
    return c


def layouts(w, scale, v_reduce, per_o, v_span, g_span, b_span):
    import numpy as np

    order = np.arange(C).reshape(C // 8, 2, GC).transpose(1, 0, 2).reshape(2, 32)
    at = np.repeat(order, 2, axis=0).reshape(128)
    p = np.zeros((128, P_N), np.float32)
    p[:, P_SCALE] = scale[at]
    for i, v in enumerate(per_o):
        p[:, P_G + i] = np.tile(v, PX)
    p[:, P_VT:P_VT + O] = v_reduce.T[at]
    p[:, P_ROW:P_CONV] = np.tile(v_reduce, (PX, 1))
    p[:, P_CONV:P_N] = w.transpose(1, 2, 3, 0)[at][..., order.reshape(C)].reshape(128, 9 * C)
    span = np.concatenate([v_span.reshape(TAPS, GROUPS * O), g_span.reshape(TAPS, GROUPS),
                           b_span.reshape(TAPS, GROUPS)], axis=1)
    gb = np.concatenate([g_span, b_span]).reshape(1, -1)
    return p, np.ascontiguousarray(span), gb, np.ascontiguousarray(v_reduce.reshape(1, -1))


def inputs_of(x, L0_conv_weight, L0_conv_scale, L1_conv_v_reduce, L1_conv_g_reduce, L1_conv_b_reduce,
              L1_conv_bn_gamma, L1_conv_bn_beta, L1_conv_bn_mean, L1_conv_bn_var, L1_conv_v_span,
              L1_conv_g_span, L1_conv_b_span):
    import numpy as np

    per_o = [np.asarray(a) for a in (L1_conv_g_reduce, L1_conv_b_reduce, L1_conv_bn_gamma, L1_conv_bn_beta,
                                     L1_conv_bn_mean, L1_conv_bn_var)]
    p, span, gb, vr = layouts(np.asarray(L0_conv_weight), np.asarray(L0_conv_scale), np.asarray(L1_conv_v_reduce),
                              per_o, np.asarray(L1_conv_v_span), np.asarray(L1_conv_g_span),
                              np.asarray(L1_conv_b_span))
    return {"x_dram": np.ascontiguousarray(x), "consts_dram": constants(), "params_dram": p, "span_dram": span,
            "gb_dram": gb, "vr_dram": vr}


def kernel(**inputs):
    import concourse.bacc as bacc
    from concourse.bass_utils import run_bass_kernel_spmd

    arrays = inputs_of(**inputs)
    nc = bacc.Bacc("TRN2", target_bir_lowering=False, num_devices=1)
    ins = [nc.dram_tensor(n, a.shape, mybir.dt.from_np(a.dtype), kind="ExternalInput").ap() for n, a in arrays.items()]
    out = nc.dram_tensor("out_dram", (B, C, H, W), F32, kind="ExternalOutput").ap()
    build(nc, *ins, out)
    r = run_bass_kernel_spmd(nc, [arrays], core_ids=[0])
    return r.results[0]["out_dram"]
```
